# Optimizing a Trainium2 kernel written in Bass

```python
import numpy as np
import jax
import jax.numpy as jnp

def _softmax(x, axis=-1):
    return jax.nn.softmax(x, axis=axis)

def _gelu(x):
    return jax.nn.gelu(x, approximate=True)

def _silu(x):
    return jax.nn.silu(x)

def _sigmoid(x):
    return jax.nn.sigmoid(x)

def _layernorm(x, axis=-1, eps=1e-05):
    m = jnp.mean(x, axis=axis, keepdims=True)
    v = jnp.var(x, axis=axis, keepdims=True)
    return (x - m) / jnp.sqrt(v + eps)

def _scatter_add(tgt, idx, src, axis=0):
    return tgt.at[idx].add(src)

def _segment_sum(src, seg, n):
    return jax.ops.segment_sum(src, seg, n)
kernel_name = 'mk_decoder_preln_d1_seqx_r2_576cad'

def setup_inputs(seed: int=0):
    np.random.seed(seed)
    _w = jnp.asarray

    def _rec_inputs():
        import jax
        import jax.numpy as jnp
        _rk = jax.random.key(seed)
        x = -0.000125 + 0.9999 * jax.random.normal(jax.random.fold_in(_rk, 1), (2, 1024, 2048), jnp.float32)
        _lenS = 1024 - jax.random.randint(jax.random.fold_in(_rk, 7), (2,), 0, max(1, 1024 // 4) + 1, jnp.int32)
        _lenS2 = 2048 - jax.random.randint(jax.random.fold_in(_rk, 8), (2,), 0, max(1, 2048 // 4) + 1, jnp.int32)
        _ctx_4096P = jax.random.normal(jax.random.fold_in(_rk, 11), (2, 16, 2048), jnp.float32)
        _ctx_4096c = jax.random.dirichlet(jax.random.fold_in(_rk, 511), 0.3 * jnp.ones((16,), jnp.float32), (2, 2048))
        _ctx_4096t = jnp.einsum('bsk,bkd->bsd', _ctx_4096c, _ctx_4096P)
        _ctx_4096t = _ctx_4096t * jax.lax.rsqrt(jnp.mean(jnp.square(_ctx_4096t)) + 1e-12) * 0.953939
        ctx_4096 = -5.72187e-05 + 0.999849 * (_ctx_4096t + 0.3 * jax.random.normal(jax.random.fold_in(_rk, 611), (2, 2048, 2048), jnp.float32))
        return (x, ctx_4096)
    x, ctx_4096 = _rec_inputs()

    def _L0_attn_setup():
        import jax, jax.numpy as jnp
        import numpy as np
        HDC_DIM = 2048
        N_HEADS = 4
        HEAD_DIM = HDC_DIM // N_HEADS

        def _ste_sign(w):
            alpha = jnp.mean(jnp.abs(w), axis=-1, keepdims=True)
            hard = alpha * jnp.sign(w)
            hard = jnp.where(hard == 0, alpha, hard)
            return jax.lax.stop_gradient(hard - w) + w
        key = jax.random.key(seed)
        kx, kq, kk, kv = jax.random.split(key, 4)
        B, T = (4, 1024)
        x = jax.random.normal(kx, (B, T, HDC_DIM), dtype=jnp.float32)
        bv_q = jax.random.normal(kq, (N_HEADS, HEAD_DIM), dtype=jnp.float32) * 0.02
        bv_k = jax.random.normal(kk, (N_HEADS, HEAD_DIM), dtype=jnp.float32) * 0.02
        bv_v = jax.random.normal(kv, (N_HEADS, HEAD_DIM), dtype=jnp.float32) * 0.02
        return {'x': x, 'bv_q': bv_q, 'bv_k': bv_k, 'bv_v': bv_v}
    _L0_attn_all = _L0_attn_setup()
    _L0_attn_in = {k: v for k, v in _L0_attn_all.items() if k in ('bv_q', 'bv_k', 'bv_v')}
    del _L0_attn_all

    def _L0_xattn_setup():
        import jax, jax.numpy as jnp
        import numpy as np
        QMIN = 0.0
        QMAX = 255.0

        def fake_quant(x, scale, zp):
            s = scale.reshape(())
            z = zp.reshape(())
            q = jnp.clip(jnp.round(x / s + z), QMIN, QMAX)
            return (q - z) * s
        key = jax.random.key(seed)
        k1, k2 = jax.random.split(key)
        B, M, K, N = (4, 1024, 2048, 2048)
        x1 = jax.random.normal(k1, (B, M, K), dtype=jnp.float32)
        x2 = jax.random.normal(k2, (B, K, N), dtype=jnp.float32)
        x1_scale = jnp.full((1,), 8.0 / 255.0, dtype=jnp.float32)
        x1_zp = jnp.full((1,), 128.0, dtype=jnp.float32)
        x2_scale = jnp.full((1,), 8.0 / 255.0, dtype=jnp.float32)
        x2_zp = jnp.full((1,), 128.0, dtype=jnp.float32)
        return {'x1': x1, 'x2': x2, 'x1_scale': x1_scale, 'x1_zp': x1_zp, 'x2_scale': x2_scale, 'x2_zp': x2_zp}
    _L0_xattn_all = _L0_xattn_setup()
    _L0_xattn_in = {k: v for k, v in _L0_xattn_all.items() if k in ('x1_scale', 'x1_zp', 'x2_scale', 'x2_zp')}
    del _L0_xattn_all

    def _L0_ffn_setup():
        import jax, jax.numpy as jnp
        import numpy as np
        HID, BOT, RDIM, NSLOT, K, VB = (2048, 64, 48, 512, 8, 128)
        TAU_LOW, TAU_HIGH, EARLY_EXIT = (0.5, 2.0, 0.05)

        def _uncertainty(h, Wu1, bu1, Wu2, bu2):
            var = jnp.var(h, axis=-1)
            log_var = jnp.log1p(var)
            norm_var = log_var / (jnp.mean(log_var) + 1e-06)
            learned = (jax.nn.gelu(h @ Wu1.T + bu1) @ Wu2.T + bu2)[..., 0]
            return jnp.clip(norm_var * 0.5 + jax.nn.sigmoid(learned) * 2.5, 0.0, 5.0)
        key = jax.random.key(seed)
        ks = jax.random.split(key, 12)
        B, S = (2, 1024)
        return {'hidden_states': jax.random.normal(ks[0], (B, S, HID), dtype=jnp.float32), 'Wq': jax.random.normal(ks[1], (BOT, HID), dtype=jnp.float32) / np.sqrt(HID), 'Wr': jax.random.normal(ks[2], (RDIM, BOT), dtype=jnp.float32) / np.sqrt(BOT), 'aux_keys': jax.random.normal(ks[3], (NSLOT, BOT), dtype=jnp.float32) * 0.01, 'aux_values': jax.random.normal(ks[4], (NSLOT, HID), dtype=jnp.float32) * 0.02, 'Wvd': jax.random.normal(ks[5], (VB, HID), dtype=jnp.float32) * 0.1 / np.sqrt(HID), 'Wvu': jax.random.normal(ks[6], (HID, VB), dtype=jnp.float32) * 0.1 / np.sqrt(VB), 'Wu1': jax.random.normal(ks[7], (HID // 4, HID), dtype=jnp.float32) / np.sqrt(HID), 'bu1': jnp.zeros((HID // 4,), dtype=jnp.float32), 'Wu2': jax.random.normal(ks[8], (1, HID // 4), dtype=jnp.float32) * 0.01, 'bu2': jnp.zeros((1,), dtype=jnp.float32), 'gate_w1': jnp.float32(0.5), 'gate_bias': jnp.float32(-1.0), 'log_rel': jnp.zeros((NSLOT,), dtype=jnp.float32)}
    _L0_ffn_all = _L0_ffn_setup()
    _L0_ffn_in = {k: v for k, v in _L0_ffn_all.items() if k in ('Wq', 'Wr', 'aux_keys', 'aux_values', 'Wvd', 'Wvu', 'Wu1', 'bu1', 'Wu2', 'bu2', 'gate_w1', 'gate_bias', 'log_rel')}
    del _L0_ffn_all
    return {'x': x, 'ctx_4096': ctx_4096, 'L0_attn_bv_q': _L0_attn_in['bv_q'], 'L0_attn_bv_k': _L0_attn_in['bv_k'], 'L0_attn_bv_v': _L0_attn_in['bv_v'], 'L0_xattn_x1_scale': _L0_xattn_in['x1_scale'], 'L0_xattn_x1_zp': _L0_xattn_in['x1_zp'], 'L0_xattn_x2_scale': _L0_xattn_in['x2_scale'], 'L0_xattn_x2_zp': _L0_xattn_in['x2_zp'], 'L0_ffn_Wq': _L0_ffn_in['Wq'], 'L0_ffn_Wr': _L0_ffn_in['Wr'], 'L0_ffn_aux_keys': _L0_ffn_in['aux_keys'], 'L0_ffn_aux_values': _L0_ffn_in['aux_values'], 'L0_ffn_Wvd': _L0_ffn_in['Wvd'], 'L0_ffn_Wvu': _L0_ffn_in['Wvu'], 'L0_ffn_Wu1': _L0_ffn_in['Wu1'], 'L0_ffn_bu1': _L0_ffn_in['bu1'], 'L0_ffn_Wu2': _L0_ffn_in['Wu2'], 'L0_ffn_bu2': _L0_ffn_in['bu2'], 'L0_ffn_gate_w1': _L0_ffn_in['gate_w1'], 'L0_ffn_gate_bias': _L0_ffn_in['gate_bias'], 'L0_ffn_log_rel': _L0_ffn_in['log_rel']}

def reference(x, ctx_4096, L0_attn_bv_q, L0_attn_bv_k, L0_attn_bv_v, L0_xattn_x1_scale, L0_xattn_x1_zp, L0_xattn_x2_scale, L0_xattn_x2_zp, L0_ffn_Wq, L0_ffn_Wr, L0_ffn_aux_keys, L0_ffn_aux_values, L0_ffn_Wvd, L0_ffn_Wvu, L0_ffn_Wu1, L0_ffn_bu1, L0_ffn_Wu2, L0_ffn_bu2, L0_ffn_gate_w1, L0_ffn_gate_bias, L0_ffn_log_rel):
    import jax
    import jax.numpy as jnp

    def _L0_attn_ref(x, bv_q, bv_k, bv_v):
        import jax, jax.numpy as jnp
        import numpy as np
        HDC_DIM = 2048
        N_HEADS = 4
        HEAD_DIM = HDC_DIM // N_HEADS

        def _ste_sign(w):
            alpha = jnp.mean(jnp.abs(w), axis=-1, keepdims=True)
            hard = alpha * jnp.sign(w)
            hard = jnp.where(hard == 0, alpha, hard)
            return jax.lax.stop_gradient(hard - w) + w
        B, T, D = x.shape
        H, HD = (N_HEADS, HEAD_DIM)
        scale = HD ** (-0.5)
        q_bind = _ste_sign(bv_q)
        k_bind = _ste_sign(bv_k)
        v_bind = _ste_sign(bv_v)
        xh = x.reshape(B, T, H, HD)
        Q = xh * q_bind
        K = xh * k_bind
        V = xh * v_bind
        scores = jnp.einsum('bthd,bshd->bhts', Q, K) * scale
        causal = jnp.tril(jnp.ones((T, T), dtype=bool))
        attn = jnp.where(causal, jax.nn.sigmoid(scores * 4.0), 0.0)
        out = jnp.einsum('bhts,bshd->bthd', attn, V)
        return out.reshape(B, T, D)

    def _L0_xattn_ref(x1, x2, x1_scale, x1_zp, x2_scale, x2_zp):
        import jax, jax.numpy as jnp
        import numpy as np
        QMIN = 0.0
        QMAX = 255.0

        def fake_quant(x, scale, zp):
            s = scale.reshape(())
            z = zp.reshape(())
            q = jnp.clip(jnp.round(x / s + z), QMIN, QMAX)
            return (q - z) * s
        q1 = fake_quant(x1, x1_scale, x1_zp)
        q2 = fake_quant(x2, x2_scale, x2_zp)
        return jnp.matmul(q1, q2)

    def _L0_ffn_ref(hidden_states, Wq, Wr, aux_keys, aux_values, Wvd, Wvu, Wu1, bu1, Wu2, bu2, gate_w1, gate_bias, log_rel):
        import jax, jax.numpy as jnp
        import numpy as np
        HID, BOT, RDIM, NSLOT, K, VB = (2048, 64, 48, 512, 8, 128)
        TAU_LOW, TAU_HIGH, EARLY_EXIT = (0.5, 2.0, 0.05)

        def _uncertainty(h, Wu1, bu1, Wu2, bu2):
            var = jnp.var(h, axis=-1)
            log_var = jnp.log1p(var)
            norm_var = log_var / (jnp.mean(log_var) + 1e-06)
            learned = (jax.nn.gelu(h @ Wu1.T + bu1) @ Wu2.T + bu2)[..., 0]
            return jnp.clip(norm_var * 0.5 + jax.nn.sigmoid(learned) * 2.5, 0.0, 5.0)
        query = hidden_states @ Wq.T
        rq = query @ Wr.T
        rk = aux_keys @ Wr.T
        router_scores = jnp.einsum('bsr,nr->bsn', rq, rk) / np.sqrt(RDIM) + log_rel
        top_scores, top_idx = jax.lax.top_k(router_scores, K)
        sel_keys = aux_keys[top_idx]
        attn = jnp.einsum('bsd,bskd->bsk', query, sel_keys) / np.sqrt(BOT) + log_rel[top_idx]
        w = jax.nn.softmax(attn, axis=-1)
        sel_vals = aux_values[top_idx]
        aux_out = jnp.einsum('bsk,bskh->bsh', w, sel_vals)
        aux_out = aux_out @ Wvd.T @ Wvu.T
        u = _uncertainty(hidden_states, Wu1, bu1, Wu2, bu2)
        u_norm = jnp.clip((u - TAU_LOW) / (TAU_HIGH - TAU_LOW), 0.0, 1.0)
        gate = jax.nn.sigmoid(gate_w1 * u_norm + gate_bias)
        gate = jnp.where(gate < EARLY_EXIT, 0.0, gate)
        return hidden_states + gate[..., None] * aux_out
    x = x + _L0_attn_ref(_layernorm(x, axis=-1), L0_attn_bv_q, L0_attn_bv_k, L0_attn_bv_v)
    x = x + _L0_xattn_ref(_layernorm(x, axis=-1), ctx_4096, L0_xattn_x1_scale, L0_xattn_x1_zp, L0_xattn_x2_scale, L0_xattn_x2_zp)
    x = x + _L0_ffn_ref(_layernorm(x, axis=-1), L0_ffn_Wq, L0_ffn_Wr, L0_ffn_aux_keys, L0_ffn_aux_values, L0_ffn_Wvd, L0_ffn_Wvu, L0_ffn_Wu1, L0_ffn_bu1, L0_ffn_Wu2, L0_ffn_bu2, L0_ffn_gate_w1, L0_ffn_gate_bias, L0_ffn_log_rel)
    return x

_drawn_inputs = setup_inputs


def setup_inputs(seed=0):
    import zlib

    import numpy as np

    out = dict(_drawn_inputs(seed))
    spreads = {'L0_ffn_bu1': (0.0, 2.0), 'L0_ffn_log_rel': (0.0, 2.0)}
    factors = {'L0_attn_bv_q': 34.363,
     'L0_attn_bv_k': 33.756,
     'L0_ffn_Wq': 64.0,
     'L0_ffn_Wr': 64.0,
     'L0_ffn_aux_keys': 64.0,
     'L0_ffn_aux_values': 64.0,
     'L0_ffn_Wvd': 64.0,
     'L0_ffn_Wvu': 64.0,
     'L0_ffn_Wu1': 64.0,
     'L0_ffn_Wu2': 64.0}
    for name, (base, spread) in spreads.items():
        noise = np.random.default_rng([zlib.crc32(name.encode()), seed]).standard_normal(out[name].shape)
        drawn = base * np.exp(spread * noise) if base else spread * noise
        out[name] = jnp.asarray(drawn.astype(out[name].dtype))
    for name, factor in factors.items():
        out[name] = (out[name] * factor).astype(out[name].dtype)
    return out
```

```python
from contextlib import ExitStack

import concourse.bass as bass
from concourse import mybir

ALU = mybir.AluOpType
ACT = mybir.ActivationFunctionType
AX = mybir.AxisListType
F32 = mybir.dt.float32
F16 = mybir.dt.float16
BF16 = mybir.dt.bfloat16
U32 = mybir.dt.uint32

P = 128
B, T, D = 2, 1024, 2048
H = 4
HD = D // H
NT = T // P
DC = HD // P
KC = D // P
NS = D // 512
RDIM, BOT, NSLOT, VB, FU = 48, 64, 512, 128, 512
SC = NSLOT // P
EPS = 1e-5
FP16_LIFT = 4096.0
MAGIC = 1.5 * 2.0 ** 23
QMID = 128.0
LOWEST = -3.0e38
FAR = -1.0e30
TG = 2
NG = B * NT // TG

PIECES = []
_at = 0
for _s in range(NT):
    for _a, _z in ((P * _s, T // 2), (max(P * _s, T // 2), T)):
        if _a < _z:
            PIECES.append((_s, _a, _z - _a, _at))
            _at += _z - _a
ACOLS = _at
NPC = len(PIECES)
PC_UNTIL = [max(i for i, p in enumerate(PIECES) if p[0] == s) + 1 for s in range(NT)]
PC_OF = [[i for i, p in enumerate(PIECES) if p[0] == s] for s in range(NT)]
STORE = [min(p[3] for p in PIECES if p[0] == s) for s in range(NT)]

V_AFTER = [[0], [1], [2], [3, 4], [5, 6], [7], [], []]
CTX_AFTER = {3: 0, 4: 1, 5: 2, 6: 3}

W_X = 0
W_V = W_X + NT * D
W_QT = W_V + NT * 2 * HD
W_KT = W_QT + DC * T
W_A = W_KT + DC * T
W_Q2 = W_A + ACOLS
W_SIG = W_Q2 + KC * HD
W_XN = W_SIG + 3 * 512
W_OT = W_XN + 2 * 512
W_VB = W_OT + 2 * 512
W_CONST = W_VB + D
W_END = W_CONST + 1900

DVE_BATCH, DVE_PAIR = 308, 32


class Order:

    def __init__(self, eng, sem):
        self.eng, self.sem, self.total, self.base, self.n = eng, sem, 0, 0, 0

    def did(self, ins):
        ins.then_inc(self.sem, 1)
        self.n += 1
        return self.n

    def wait(self, at=None):
        self.eng.wait_ge(self.sem, self.base + (self.n if at is None else at))

    def link(self, ins):
        self.did(ins)
        self.wait()

    def enter(self, turn, per):
        self.base, self.n = self.total + turn * per, 0

    def leave(self, turns, per):
        assert self.n == per, f"count a turn: {self.n}, not {per}"
        self.total += turns * per
        self.base, self.n = self.total, 0

    def start(self):
        self.total += self.n
        self.base, self.n = self.total, 0


def decoder_kernel(nc, x, ctx, bv_q, bv_k, bv_v, s1, z1, s2, z2, wq, wr, aux_k, aux_v, wvd, wvu,
                   wu1, bu1, wu2, bu2, gate_w1, gate_bias, log_rel, out):
    x_r = x.rearrange("b (t p) d -> (b t) p d", p=P)
    out_r = out.rearrange("b (t p) d -> (b t) p d", p=P)
    ctx_r = ctx.rearrange("b (j k p) (s n) -> j s b p k n", p=P, k=4, n=512)
    x2_d = nc.dram_tensor("x2_spill", (B * NT, P, D), F32, kind="Internal").ap()
    wt_d = nc.dram_tensor("wu1_split", (P, 4, 2 * KC * P), F16, kind="Internal").ap()
    wqt_d = nc.dram_tensor("wq_split", (P, 2, KC, BOT), F16, kind="Internal").ap()
    wvut_d = nc.dram_tensor("wvu_split", (P, 2 * D), F16, kind="Internal").ap()
    s65_d = nc.dram_tensor("score_rhs", (BOT + 1, 2 * NSLOT), F32, kind="Internal").ap()

    es = ExitStack()
    with es:
        es.enter_context(nc.allow_non_contiguous_dma("small vectors are laid out by partition"))

        def sem(name):
            return es.enter_context(nc.semaphore(name))

        arena = es.enter_context(nc.sbuf_tensor("arena", [P, W_END], F32))
        banks = [es.enter_context(nc.psum_tensor(f"bank{i}", [P, 512], F32))[:, :] for i in range(8)]

        def view(word, words, dt=F32):
            ap = arena[:, word:word + words]
            return ap if dt is F32 else ap.bitcast(dt)

        free = [W_CONST]

        def small(words, dt=F32):
            free[0] += words
            assert free[0] <= W_END
            return view(free[0] - words, words, dt)

        identf, onesf, mask = small(P), small(P), small(P)
        ident16, identb = small(P // 2, F16), small(P // 2, BF16)
        ones16, onesb = small(P // 2, F16), small(1, BF16)
        m1 = small(SC * VB).rearrange("p (c v) -> p c v", c=SC)
        qp = small(10)
        S1, Z1, S2, Z2, R1S, R2S, S12, ND2, ND1, KDD = [qp[:, i:i + 1] for i in range(10)]
        alpha = small(4 * H).rearrange("p (k h) -> p k h", h=H)
        part = small(2 * H).rearrange("p (k h) -> p k h", h=H)
        bqk = small(2 * H * DC).rearrange("p (k h c) -> p k h c", k=2, h=H)
        sgn = small(2 * H * DC).rearrange("p (k h c) -> p k h c", k=2, h=H)
        btm = small(2 * H * DC).rearrange("p (k h c) -> p k h c", k=2, h=H)
        bnd = small(2 * H * DC).rearrange("p (k h c) -> p k h c", k=2, h=H)
        rse = small(3 * H * DC).rearrange("p (k h c) -> p k h c", k=3, h=H)
        sigscale = small(H)
        mx = small(8)
        mx3, gm3, pw3, scl3, uns3 = small(4), small(4), small(4), small(4), small(4)
        bn = small(NT * 4 * 6).rearrange("p (t s k) -> p t s k", t=NT, s=4)
        mv = small(NT * 2).rearrange("p (t k) -> p t k", k=2)
        rstd, veps, sdev, nwt = small(NT), small(NT), small(NT), small(NT)
        vh = small(NT)
        mv1_t = small(NT * 2).rearrange("p (t k) -> p t k", k=2)
        rstd1_t = small(NT)
        cvec = small(NT)
        tab = small(3 * B * NT).rearrange("p (k t) -> p k t", k=3)
        logv, lsum, lmean = small(B * NT), small(1), small(1)
        bu1s, wu2s, hbu2, gw = small(4), small(4), small(1), small(2)
        gsc = small(1)
        cur = small(2 * 3 * TG).rearrange("p (q k t) -> p q k t", q=2, k=3)
        m8 = small(2 * 8).rearrange("p (t k) -> p t k", k=8)
        nmx, den, rden = small(2), small(2), small(2)
        ge = small(10 * TG).rearrange("p (k t) -> p k t", t=TG)
        pause = small(1, U32)

        X = view(W_X, NT * D).rearrange("p (t d) -> p t d", t=NT)
        V = view(W_V, NT * 2 * HD, F16).rearrange("p (q t l d) -> p q t l d", q=2, t=NT, l=2)
        QT = view(W_QT, DC * T, F16).rearrange("p (l c t) -> p l c t", l=2, c=DC)
        KT = view(W_KT, DC * T, F16).rearrange("p (l c t) -> p l c t", l=2, c=DC)
        A = view(W_A, ACOLS, F16).rearrange("p (l t) -> p l t", l=2)
        sig = view(W_SIG, 3 * 512).rearrange("p (q n) -> p q n", q=3)
        xn = view(W_XN, 2 * 512).rearrange("p (q n) -> p q n", q=2)
        ktmp = view(W_XN, 2 * 512, F16).rearrange("p (q n) -> p q n", q=2)
        otmp = view(W_OT, 2 * 512).rearrange("p (q n) -> p q n", q=2)
        vb = view(W_VB, D).rearrange("p (h d) -> p h d", h=H)
        Q2 = view(W_Q2, KC * HD, BF16).rearrange("p (q k n) -> p q k n", q=2, k=KC)
        xq = view(W_Q2 + KC * HD // 2, 2 * D).rearrange("p (q d) -> p q d", q=2)
        q1b = view(W_QT + DC * T // 2, D, BF16).rearrange("p (q d) -> p q d", q=2)
        tree = view(W_QT, DC * T // 2, F16).rearrange("p (k n) -> p k n", n=512)
        raw = view(W_V, 2 * D).rearrange("p (q k n) -> p q k n", q=2, k=4)
        q1T = view(W_KT, NT * D // 2, BF16).rearrange("p (t k n) -> p t k n", t=NT, k=KC)
        cb = otmp

        wu_in = view(W_V, 4 * D).rearrange("p (f d) -> p f d", f=4)
        wq_in = view(W_QT, D)
        wvu_in = view(W_QT + D, D).rearrange("p (k v) -> p k v", v=VB)
        wvd_in = view(W_KT, D)
        wvdT = view(W_KT + D, D).rearrange("p (k v) -> p k v", v=VB)
        split = view(W_A, 2 * D, F16).rearrange("p (q l d) -> p q l d", q=2, l=2)
        av_in = view(W_A + 2 * D, 4 * D).rearrange("p (s d) -> p s d", s=4)
        avT = view(W_V, 4 * D).rearrange("p (s k n) -> p s k n", s=4, k=KC)
        s65p = view(W_SIG, 2 * NSLOT)
        ak_in = view(W_SIG + 1024, SC * BOT).rearrange("p (c d) -> p c d", c=SC)
        akT = view(W_SIG + 1280, NSLOT)
        rkT = view(W_SIG + 1792, NSLOT)
        wr_in, wrT = view(W_SIG + 2304, BOT), view(W_SIG + 2368, RDIM)

        Y = view(0, 2 * TG * D).rearrange("p (q t d) -> p q t d", q=2, t=TG)
        hT = view(4 * D, 4 * D, F16).rearrange("p (q l k t) -> p q l k t", q=2, l=2, k=KC)
        WT = view(W_V, 4 * D, F16).rearrange("p (f l k n) -> p f l k n", f=4, l=2, k=KC)
        WQT = view(W_QT, KC * BOT, F16).rearrange("p (l k n) -> p l k n", l=2, k=KC)
        WVUT = view(W_QT + KC * BOT, D, F16).rearrange("p (l d) -> p l d", l=2)
        s65 = view(W_QT + KC * BOT + D, 2 * NSLOT)
        hs = view(W_KT, TG * D).rearrange("p (t d) -> p t d", t=TG)
        w0 = W_KT + TG * D
        gl = view(w0, 512).rearrange("p (q t) -> p q t", q=2)
        qT = view(w0 + 512, 512).rearrange("p (q t) -> p q t", q=2)
        rep = view(w0 + 1024, 512)
        am = view(w0 + 1536, 1024).rearrange("p (t n) -> p t n", t=2)
        ew = view(w0 + 2560, 1024).rearrange("p (t n) -> p t n", t=2)
        nsel = view(w0 + 3584, 512)
        wTt = view(w0 + 4096, 1024).rearrange("p (c t) -> p c t", c=SC)
        low = view(w0 + 5120, 256, F16).rearrange("p (l t) -> p l t", l=2)
        lrow = view(w0 + 5376, 256)
        F = view(w0 + 5632, 2 * TG * D).rearrange("p (q t d) -> p q t d", q=2, t=TG)

        TPH = [banks[0][:, :].bitcast(F16), banks[2][:, :].bitcast(F16)]
        TPL = [banks[1][:, :].bitcast(F16), banks[3][:, :].bitcast(F16)]
        TQ = [[banks[2 * i + j][:, :].bitcast(BF16).rearrange("p (k n) -> p k n", k=8) for j in range(2)]
              for i in range(2)]
        SB = [banks[4], banks[5]]
        PO = [banks[6], banks[7]]
        quad = [banks[i][:, :].rearrange("p (k n) -> p k n", k=4) for i in range(8)]

        consts_made = sem("consts_made")
        consts_cast = sem("consts_cast")
        small_in = sem("small_in")
        wu_ld = [sem(f"wu_ld{i}") for i in range(4)]
        wq_ld, wvu_ld, wvd_ld = sem("wq_ld"), sem("wvu_ld"), sem("wvd_ld")
        av_ld = [sem(f"av_ld{i}") for i in range(4)]
        abs_done, absmax_all = sem("abs_done"), sem("absmax_all")
        scales_ready = sem("scales_ready")
        quad_ready, quad_hi, quad_used = sem("quad_ready"), sem("quad_hi"), sem("quad_used")
        split_stored = [sem(f"split_stored{i}") for i in range(2)]
        bv_part, bv_sum = sem("bv_part"), sem("bv_sum")
        ak_tr, ak_copied, rk_ready, rk_copied, m2_ready = (sem("ak_tr"), sem("ak_copied"), sem("rk_ready"),
                                                           sem("rk_copied"), sem("m2_ready"))
        s65_made, s65_row, s65_stored = sem("s65_made"), sem("s65_row"), sem("s65_stored")
        m1_ready = sem("m1_ready")
        prep_done, wq_stored = sem("prep_done"), sem("wq_stored")

        x_loaded = [sem(f"x_loaded{t}") for t in range(NT)]
        ctx_loaded = [sem(f"ctx_loaded{q}") for q in range(2)]
        x2_stored = [sem(f"x2_stored{t}") for t in range(NT)]
        veps_ready, sdev_ready = sem("veps_ready"), sem("sdev_ready")
        xn_ready, vhi_ready, v_ready = sem("xn_ready"), sem("vhi_ready"), sem("v_ready")
        tr_ready, qhi_ready, kt_ready = sem("tr_ready"), sem("qhi_ready"), sem("kt_ready")
        scores_ready, sig_ready, attn_ready = sem("scores_ready"), sem("sig_ready"), sem("attn_ready")
        out_ready, out_used, x1_ready = sem("out_ready"), sem("out_used"), sem("x1_ready")
        xq_ready, xqz_ready, q1_ready = sem("xq_ready"), sem("xqz_ready"), sem("q1_ready")
        q1tr_ready, q1ta_ready, q1td_ready, rows_ready = (sem("q1tr_ready"), sem("q1ta_ready"),
                                                          sem("q1td_ready"), sem("rows_ready"))
        ctx_scaled, raw_used, q2_ready = sem("ctx_scaled"), sem("raw_used"), sem("q2_ready")
        cols_ready, cb_ready, rows_used = sem("cols_ready"), sem("cb_ready"), sem("rows_used")
        mm_ready, mm_used, x2_ready, x2_counted = sem("mm_ready"), sem("mm_used"), sem("x2_ready"), sem("x2_counted")

        w3_loaded = sem("w3_loaded")
        tab_ready, log_ready, lsum_ready, lsum_all = sem("tab_ready"), sem("log_ready"), sem("lsum_ready"), sem("lsum_all")
        y_loaded = [sem(f"y_loaded{q}") for q in range(4)]
        h_ready, y_ready = sem("h_ready"), sem("y_ready")
        ht_tr, ht_hi, ht_ready = sem("ht_tr"), sem("ht_hi"), sem("ht_ready")
        q_ready, qT_ready, sc_ready, sc_used = sem("q_ready"), sem("qT_ready"), sem("sc_ready"), sem("sc_used")
        nmx_ready, e_ready, w_ready = sem("nmx_ready"), sem("e_ready"), sem("w_ready")
        u_ready, gelu_ready, lrn_ready, lrow_ready, lcol_ready = (sem("u_ready"), sem("gelu_ready"), sem("lrn_ready"),
                                                                  sem("lrow_ready"), sem("lcol_ready"))
        e1_ready, z_ready, e2_ready = sem("e1_ready"), sem("z_ready"), sem("e2_ready")
        wT_tr, wT_ready, low_mm, low_hi, low_ready = (sem("wT_tr"), sem("wT_ready"), sem("low_mm"), sem("low_hi"),
                                                      sem("low_ready"))
        fin_ready, fin_used = sem("fin_ready"), sem("fin_used")
        stored = [sem(f"stored{q}") for q in range(4)]
        dve_order, pool_order = sem("dve_order"), sem("pool_order")

        N_SMALL = 16

        block = es.enter_context(nc.Block())


        @block.sync
        def _(sp):
            for t in range(NT):
                sp.sem_inc(x2_stored[t], 1)
            for q in range(4):
                sp.sem_inc(stored[q], 1)
            with sp.Fori(0, B) as b:
                for t in range(NT):
                    sp.wait_ge(x2_stored[t], 16 * b + 1)
                    sp.dma_start(X[:, t, :], x_r[bass.ds(b * NT + t, 1)].rearrange("a p d -> p (a d)"))\
                      .then_inc(x_loaded[t], 16)
                sp.wait_ge(out_ready, 32 * b + 24)
                for s in range(NS):
                    for j in range(4):
                        if s or j >= 2:
                            sp.wait_ge(raw_used, 16 * b + 4 * s + j - 1)
                        sp.dma_start(raw[:, j % 2],
                                     ctx_r[j, s, bass.ds(b, 1)].rearrange("a p k n -> p (a k) n"))\
                          .then_inc(ctx_loaded[j % 2], 16)
                for t in range(NT):
                    sp.wait_ge(x2_counted, 8 * b + t + 2)
                    sp.dma_start(x2_d[bass.ds(b * NT + t, 1)].rearrange("a p d -> p (a d)"), X[:, t, :])\
                      .then_inc(x2_stored[t], 16)

            def store(n, q):
                for t in range(TG):
                    sp.wait_ge(fin_used, 8 * n + 4 * t + 5)
                    sp.dma_start(out_r[bass.ds(n * TG + t, 1)].rearrange("a p d -> p (a d)"), F[:, q, t, :])\
                      .then_inc(stored[2 * q + t], 16)

            with sp.Fori(0, NG // 2) as i:
                for q in range(2):
                    store(2 * i + q, q)
            for q in range(4):
                sp.wait_ge(stored[q], 16 * (NG // 2) + 1)

        @block.gpsimd
        def _(pool):
            order = Order(pool, pool_order)
            pool.sem_inc(y_ready, 1)
            pool.memset(onesf, 1.0).then_inc(consts_made, 1)
            order.did(pool.memset(identf, 0.0))
            order.did(pool.memset(mask, 1.0))
            order.wait()
            pool.affine_select(out=identf, in_=identf, compare_op=ALU.not_equal, fill=1.0, base=0,
                               pattern=[[-1, P]], channel_multiplier=1).then_inc(consts_made, 1)
            pool.affine_select(out=mask, in_=mask, compare_op=ALU.is_ge, fill=0.0, base=0,
                               pattern=[[1, P]], channel_multiplier=-1).then_inc(consts_made, 1)
            pool.wait_ge(abs_done, 1)
            pool.partition_all_reduce(gm3[:, 0:3], mx3[:, 0:3], P, bass.bass_isa.ReduceOp.max)\
                .then_inc(absmax_all, 1)
            for blk in range(6):
                pool.wait_ge(quad_used, 4 * blk + 4)
                src = split[:, blk % 2]
                if blk < 4:
                    dst, src = wt_d[:, blk, :], src.rearrange("p l d -> p (l d)")
                elif blk == 4:
                    dst = wqt_d
                    src = src.rearrange("p l (k n) -> p l k n", k=KC)[:, :, :, 0:BOT]
                else:
                    dst, src = wvut_d, src.rearrange("p l d -> p (l d)")
                if blk == 4:
                    for l in range(2):
                        pool.dma_start(dst[:, l], src[:, l]).then_inc(split_stored[0] if l else wq_stored, 16)
                else:
                    pool.dma_start(dst, src).then_inc(split_stored[blk % 2], 16)
            pool.wait_ge(s65_made, 2)
            pool.wait_ge(s65_row, 32)
            pool.dma_start(s65_d, s65p[0:BOT + 1, :]).then_inc(s65_stored, 16)
            pool.wait_ge(abs_done, 2)
            pool.partition_all_reduce(gm3[:, 3:4], mx3[:, 3:4], P, bass.bass_isa.ReduceOp.max)\
                .then_inc(absmax_all, 1)

            pool.wait_ge(raw_used, 16 * B)
            pool.wait_ge(cols_ready, NS * B)
            pool.wait_ge(wq_stored, 16)
            for q in range(2):
                pool.wait_ge(split_stored[q], 16 * 3)
            pool.wait_ge(s65_stored, 16)
            pool.dma_start(WQT, wqt_d).then_inc(w3_loaded, 16)
            pool.dma_start(s65[0:BOT + 1, :], s65_d).then_inc(w3_loaded, 16)
            pool.dma_start(WT.rearrange("p f l k n -> p f (l k n)"), wt_d).then_inc(w3_loaded, 16)
            pool.dma_start(WVUT.rearrange("p l d -> p (l d)"), wvut_d).then_inc(w3_loaded, 16)

            def load(n, q):
                for t in range(TG):
                    pool.dma_start(Y[:, q, t, :], x2_d[bass.ds(n * TG + t, 1)].rearrange("a p d -> p (a d)"))\
                        .then_inc(y_loaded[2 * q + t], 16)

            def add_h(n, q):
                for t in range(TG):
                    pool.wait_ge(h_ready, TG * n + t + 1)
                    pool.wait_ge(stored[2 * q + t], results_out(n))
                    pool.tensor_tensor(F[:, q, t, :], Y[:, q, t, :], hs[:, t, :], ALU.add).then_inc(y_ready, 1)

            for t in range(2 * TG):
                pool.wait_ge(x2_stored[t], 16 * B + 1)
            load(0, 0)
            load(1, 1)
            for t in range(2 * TG, NT):
                pool.wait_ge(x2_stored[t], 16 * B + 1)
            with pool.Fori(0, NG // 2 - 1) as i:
                for q in range(2):
                    results_out = lambda n: 16 * i + 1
                    add_h(2 * i + q, q)
                    pool.wait_ge(y_ready, 2 * TG * i + TG * q + TG + 1)
                    load(2 * i + q + 2, q)
            results_out = lambda n: 16 * (n // 2) + 1
            add_h(NG - 2, 0)
            add_h(NG - 1, 1)

        @block.scalar
        def _(act):
            for f in range(4):
                act.dma_start(wu_in[:, f, :], wu1[f * P:(f + 1) * P, :]).then_inc(wu_ld[f], 16)
            act.dma_start(wq_in[0:BOT, :], wq).then_inc(wq_ld, 16)
            act.dma_start(wvu_in, wvu.rearrange("(k p) v -> p k v", p=P)).then_inc(wvu_ld, 16)
            for i, h in enumerate((bv_q, bv_k)):
                for hh in range(H):
                    act.dma_start(bqk[:, i, hh, :], h[hh].rearrange("(c p) -> p c", p=P)).then_inc(small_in, 16)
            act.dma_start(vb, bv_v.partition_broadcast(P)).then_inc(small_in, 16)
            for i, a in enumerate((s1, z1, s2, z2)):
                act.dma_start(qp[:, i:i + 1], a.partition_broadcast(P)).then_inc(small_in, 16)
            act.dma_start(bu1s, bu1.rearrange("(c p) -> p c", p=P)).then_inc(small_in, 16)
            act.dma_start(wu2s, wu2.rearrange("a (c p) -> p (a c)", p=P)).then_inc(small_in, 16)
            act.dma_start(hbu2, bu2.partition_broadcast(P)).then_inc(small_in, 16)
            act.dma_start(gw[:, 0:1], gate_w1.partition_broadcast(P)).then_inc(prep_done, 16)
            act.dma_start(gw[:, 1:2], gate_bias.partition_broadcast(P)).then_inc(prep_done, 16)
            act.dma_start(wvd_in, wvd).then_inc(wvd_ld, 16)
            act.dma_start(wr_in[0:RDIM, :], wr).then_inc(prep_done, 16)
            act.dma_start(ak_in, aux_k.rearrange("(c p) d -> p c d", p=P)).then_inc(prep_done, 16)
            for s in range(4):
                act.dma_start(av_in[:, s, :], aux_v[s * P:(s + 1) * P, :]).then_inc(av_ld[s], 16)
            act.dma_start(s65p[BOT:BOT + 1, 0:NSLOT], log_rel.rearrange("(a n) -> a n", a=1)).then_inc(s65_row, 16)
            act.dma_start(s65p[BOT:BOT + 1, NSLOT:], log_rel.rearrange("(a n) -> a n", a=1)).then_inc(s65_row, 16)

            act.wait_ge(scales_ready, 1)
            for blk in range(6):
                if blk >= 2:
                    act.wait_ge(split_stored[blk % 2], 16 * (blk // 2))
                w = BOT if blk == 4 else P
                kind = 0 if blk < 4 else blk - 3
                for i in range(4):
                    q = 4 * blk + i
                    act.wait_ge(quad_ready, q + 1)
                    dst = split[:, blk % 2, 0].rearrange("p (k n) -> p k n", k=KC)[:, 4 * i:4 * i + 4, 0:w]
                    nc.scalar.activation(dst, quad[q % 4][:, :, 0:w], ACT.Copy, scale=scl3[:, kind:kind + 1])\
                        .then_inc(quad_hi, 1)

            with act.Fori(0, B) as b:
                def deviation(k, n):
                    act.wait_ge(veps_ready, 5 * b + k + 1)
                    nc.scalar.activation(sdev[:, 0:n], veps[:, 0:n], ACT.Sqrt).then_inc(sdev_ready, 1)

                def value_high(h, t):
                    act.wait_ge(xn_ready, 32 * b + 8 * h + t + 1)
                    nc.scalar.activation(V[:, h % 2, t, 0, :], xn[:, t % 2, :], ACT.Copy).then_inc(vhi_ready, 1)

                def query_high(h, c):
                    act.wait_ge(tr_ready, 16 * b + 4 * h + c + 1)
                    nc.scalar.activation(QT[:, 0, c, :], TPH[c % 2], ACT.Copy).then_inc(qhi_ready, 1)

                def sigmoids(h, s):
                    for k in PC_OF[s]:
                        act.wait_ge(scores_ready, 48 * b + NPC * h + k + 1)
                        if h == 0 and k < 3:
                            act.wait_ge(attn_ready, 48 * b + 1)
                        else:
                            act.wait_ge(attn_ready, 48 * b + NPC * h + k - 1)
                        n = PIECES[k][2]
                        nc.scalar.activation(sig[:, k % 3, 0:n], SB[k % 2][:, 0:n], ACT.Sigmoid,
                                             scale=sigscale[:, h:h + 1]).then_inc(sig_ready, 1)

                def scale_ctx(s, j):
                    act.wait_ge(ctx_loaded[j % 2], 16 * (2 * (4 * b + s) + j // 2 + 1))
                    nc.scalar.activation(raw[:, j % 2], raw[:, j % 2], ACT.Identity, bias=Z2, scale=R2S)\
                        .then_inc(ctx_scaled, 1)

                def scale_x(t):
                    act.wait_ge(xq_ready, 8 * b + t + 1)
                    nc.scalar.activation(xq[:, t % 2, :], xq[:, t % 2, :], ACT.Identity, bias=Z1, scale=R1S)\
                        .then_inc(xqz_ready, 1)

                def half_x(t):
                    act.wait_ge(q1tr_ready, 8 * b + t + 1)
                    nc.scalar.activation(q1T[:, t, 0:8, :], TQ[t % 2][0], ACT.Copy).then_inc(q1ta_ready, 1)

                deviation(0, 4)
                deviation(1, 4)
                for t in range(NT):
                    value_high(0, t)
                for c in range(DC):
                    query_high(0, c)
                for h in range(H):
                    last = h == H - 1
                    for s in range(NT):
                        sigmoids(h, s)
                        if not last:
                            for t in V_AFTER[s]:
                                value_high(h + 1, t)
                        elif s in CTX_AFTER:
                            scale_ctx(0, CTX_AFTER[s])
                    if not last:
                        for c in range(DC):
                            query_high(h + 1, c)
                deviation(2, 4)
                scale_x(0)
                scale_x(1)
                deviation(3, 4)
                for t in range(NT + 1):
                    if 2 <= t + 2 < NT:
                        scale_x(t + 2)
                    if t >= 1:
                        half_x(t - 1)
                for s in range(1, NS):
                    for j in range(4):
                        scale_ctx(s, j)
                deviation(4, NT)

            def high(n, q, g):
                act.wait_ge(ht_tr, 8 * n + g + 2)
                t, k = g // 4, g % 4
                nc.scalar.activation(hT[:, q, 0, 4 * k:4 * k + 4, t * P:(t + 1) * P], quad[g % 2], ACT.Copy)\
                    .then_inc(ht_hi, 1)

            for t in range(2 * TG, NT):
                act.wait_ge(x2_stored[t], 16 * B + 1)
            for g in range(8):
                high(0, 0, g)
            act.wait_ge(tab_ready, B)
            nc.scalar.activation(logv, tab[:, 2, :], ACT.Ln, bias=onesf[:, 0:1]).then_inc(log_ready, 1)

            def gelu(n, f):
                act.wait_ge(u_ready, 4 * n + f + 1)
                nc.scalar.activation(gl[:, f % 2, :], banks[3 - f % 2][:, 0:TG * P], ACT.Gelu_apprx_tanh,
                                     bias=bu1s[:, f:f + 1], scale=uns3[:, 0:1]).then_inc(gelu_ready, 1)

            def expo(n, t):
                act.wait_ge(nmx_ready, TG * n + t + 1)
                nc.scalar.activation(ew[:, t, :], am[:, t, :], ACT.Exp, bias=nmx[:, t:t + 1],
                                     accum_out=den[:, t:t + 1]).then_inc(e_ready, 1)

            def gate_and_low(n):
                act.wait_ge(lcol_ready, n + 1)
                nc.scalar.activation(ge[:, 0, :], banks[7][:, 300:300 + TG], ACT.Tanh, scale=0.5,
                                     bias=hbu2).then_inc(e1_ready, 1)
                act.wait_ge(z_ready, n + 1)
                nc.scalar.activation(ge[:, 6, :], ge[:, 5, :], ACT.Tanh, scale=0.5).then_inc(e2_ready, 1)
                act.wait_ge(low_mm, n + 1)
                nc.scalar.activation(low[:, 0, :], banks[7][:, 0:TG * P], ACT.Copy, scale=FP16_LIFT)\
                    .then_inc(low_hi, 1)

            def group(n, q, first, last):
                act.wait_ge(q_ready, n + 1)
                nc.scalar.activation(qT[0:BOT, q, :], banks[2][0:BOT, 0:TG * P], ACT.Copy,
                                     scale=uns3[0:BOT, 1:2]).then_inc(qT_ready, 1)
                if not first:
                    gate_and_low(n - 1)
                for f in range(4):
                    if f < 2:
                        act.wait_ge(lrn_ready, 4 * n + 1)
                    else:
                        act.wait_ge(lrn_ready, 4 * n + f)
                    gelu(n, f)
                    if f % 2:
                        expo(n, f // 2)
                    if f < 2 and not last:
                        for g in range(4 * f, 4 * f + 4):
                            high(n + 1, 1 - q, g)

            group(0, 0, True, False)
            with act.Fori(0, NG // 2 - 1) as i:
                group(2 * i + 1, 1, False, False)
                group(2 * i + 2, 0, False, False)
            group(NG - 1, 1, False, True)
            gate_and_low(NG - 1)

        @block.tensor
        def _(pe):
            pe.sem_inc(ht_tr, 1)
            pe.sem_inc(lrn_ready, 1)
            pe.wait_ge(consts_made, 3)
            pe.wait_ge(consts_cast, 4)
            pe.wait_ge(bv_part, 1)
            nc.tensor.matmul(banks[7][:, 0:2 * H], onesf, part.rearrange("p k h -> p (k h)"), start=True, stop=True)\
                .then_inc(bv_sum, 1)
            blocks = [(wu_ld[f], wu_in[:, f, :], P) for f in range(4)] + [(wq_ld, wq_in, BOT), (wvu_ld, None, P),
                      (wvd_ld, wvd_in, P)] + [(av_ld[s], av_in[:, s, :], P) for s in range(4)]
            for blk, (loaded, src, rows) in enumerate(blocks):
                pe.wait_ge(loaded, 16)
                for i in range(4):
                    q = 4 * blk + i
                    if q >= 4:
                        pe.wait_ge(quad_used, q - 3)
                    for k in range(4 * i, 4 * i + 4):
                        chunk = wvu_in[:, k, :] if src is None else src[0:rows, k * P:(k + 1) * P]
                        last = nc.tensor.transpose(quad[q % 4][:, k % 4, 0:rows], chunk, identf[0:rows, 0:rows])
                    last.then_inc(quad_ready, 1)
            pe.wait_ge(prep_done, 16 * 4)
            for c in range(SC):
                nc.tensor.transpose(banks[5][0:BOT, c * P:(c + 1) * P], ak_in[:, c, :], identf)
            nc.tensor.transpose(banks[4][0:BOT, 0:RDIM], wr_in[0:RDIM, :], identf[0:RDIM, 0:RDIM]).then_inc(ak_tr, 1)
            pe.wait_ge(ak_copied, 2)
            nc.tensor.matmul(banks[6][0:RDIM, :], wrT[0:BOT, 0:RDIM], akT[0:BOT, :], start=True, stop=True)\
                .then_inc(rk_ready, 1)
            pe.wait_ge(rk_copied, 1)
            nc.tensor.matmul(banks[7][0:BOT, :], wr_in[0:RDIM, :], rkT[0:RDIM, :], start=True, stop=True)\
                .then_inc(m2_ready, 1)
            pe.wait_ge(quad_used, 44)
            pe.wait_ge(s65_made, 2)
            for s in range(SC):
                for k in range(KC):
                    last = nc.tensor.matmul(banks[4 + s][:, 0:VB], avT[:, s, k, :], wvdT[:, k, :],
                                            start=k == 0, stop=k == KC - 1)
                last.then_inc(m1_ready, 1)

            with pe.Fori(0, B) as b:
                def turn(h, c):
                    if c == 0:
                        pe.wait_ge(v_ready, 32 * b + 8 * h + 8 + 1)
                    if c >= 2:
                        pe.wait_ge(kt_ready, 16 * b + 4 * h + c )
                    for l, bank in ((0, TPH), (1, TPL)):
                        for t in range(NT):
                            last = nc.tensor.transpose(bank[c % 2][:, t * P:(t + 1) * P],
                                                       V[:, h % 2, t, l, c * P:(c + 1) * P], ident16)
                    last.then_inc(tr_ready, 1)

                def scores(h, s):
                    for k in PC_OF[s]:
                        _, a, n, _ = PIECES[k]
                        if h == 0 and k < 2:
                            pe.wait_ge(mm_used, 32 * b + 1)
                        else:
                            pe.wait_ge(sig_ready, 48 * b + NPC * h + k - 1)
                        for c in range(DC):
                            if k == 0:
                                pe.wait_ge(kt_ready, 16 * b + 4 * h + c + 2)
                            for i, (lk, lq) in enumerate(((0, 0), (0, 1), (1, 0))):
                                last = nc.tensor.matmul(SB[k % 2][:, 0:n], KT[:, lk, c, s * P:(s + 1) * P],
                                                        QT[:, lq, c, a:a + n], start=c == 0 and i == 0,
                                                        stop=c == DC - 1 and i == 2)
                        last.then_inc(scores_ready, 1)

                def values(h, t):
                    pe.wait_ge(attn_ready, 48 * b + NPC * h + PC_UNTIL[t] + 1)
                    if h == 0 and t < 2:
                        pe.wait_ge(mm_used, 32 * b + 1)
                    else:
                        pe.wait_ge(out_used, 32 * b + 8 * h + t - 1)
                    for s in range(t + 1):
                        a = STORE[s] + (t - s) * P
                        for i, (la, lv) in enumerate(((0, 0), (0, 1), (1, 0))):
                            last = nc.tensor.matmul(PO[t % 2], A[:, la, a:a + P], V[:, h % 2, s, lv, :],
                                                    start=s == 0 and i == 0, stop=s == t and i == 2)
                    last.then_inc(out_ready, 1)

                def turn_x(t):
                    pe.wait_ge(q1_ready, 8 * b + t + 1)
                    if t >= 2:
                        pe.wait_ge(q1ta_ready, 8 * b + t - 1)
                        pe.wait_ge(q1td_ready, 8 * b + t - 1)
                    for k in range(KC):
                        last = nc.tensor.transpose(TQ[t % 2][k // 8][:, k % 8, :], q1b[:, t % 2, k * P:(k + 1) * P],
                                                   identb)
                    last.then_inc(q1tr_ready, 1)

                def row_sums(t):
                    pe.wait_ge(q1ta_ready, 8 * b + t + 1)
                    pe.wait_ge(q1td_ready, 8 * b + t + 1)
                    if t == 0:
                        pe.wait_ge(out_used, 32 * b + 32)
                    pe.wait_ge(rows_used, 8 * b + t + 1)
                    for k in range(KC):
                        last = nc.tensor.matmul(PO[0][:, t:t + 1], q1T[:, t, k, :], onesb[:, 0:1],
                                                start=k == 0, stop=k == KC - 1)
                    last.then_inc(rows_ready, 1)

                def col_sums(s):
                    pe.wait_ge(q2_ready, 4 * b + s + 1)
                    pe.wait_ge(cb_ready, 4 * b + s + 1)
                    nc.tensor.matmul(PO[1], ones16, tree[:, 0, :], start=True, stop=True).then_inc(cols_ready, 1)

                def product(s, t):
                    if s or t >= 2:
                        pe.wait_ge(mm_used, 32 * b + 8 * s + t )
                    for k in range(KC):
                        last = nc.tensor.matmul(SB[t % 2], q1T[:, t, k, :], Q2[:, s % 2, k, :],
                                                start=k == 0, stop=k == KC - 1)
                    last.then_inc(mm_ready, 1)

                for c in range(DC):
                    turn(0, c)
                for h in range(H):
                    scores(h, 0)
                    scores(h, 1)
                    for s in range(2, NT):
                        scores(h, s)
                        values(h, s - 2)
                    if h < H - 1:
                        turn(h + 1, 0)
                        turn(h + 1, 1)
                        values(h, 6)
                        turn(h + 1, 2)
                        turn(h + 1, 3)
                        values(h, 7)
                    else:
                        values(h, 6)
                        values(h, 7)
                for t in range(NT + 2):
                    if t < NT:
                        turn_x(t)
                    if 1 <= t <= NT:
                        row_sums(t - 1)
                    if t == 2:
                        col_sums(0)
                    if t >= 2:
                        product(0, t - 2)
                for s in range(1, NS):
                    col_sums(s)
                    for t in range(NT):
                        product(s, t)

            def turn_h(n, g, settled=False):
                t, k = g // 4, g % 4
                if g == 0 and not settled:
                    pe.wait_ge(mm_used, 32 * B + 1)
                pe.wait_ge(h_ready, TG * n + t + 1)
                if g >= 2:
                    pe.wait_ge(ht_ready, 8 * n + g - 1)
                elif settled:
                    pe.wait_ge(fin_used, 8 * (n - 1) + 1)
                for i in range(4):
                    kk = 4 * k + i
                    last = nc.tensor.transpose(quad[g % 2][:, i, :], hs[:, t, kk * P:(kk + 1) * P], identf)
                last.then_inc(ht_tr, 1)

            def project(n, q, f, quads=(), settled=True):
                bank, m = (banks[2], BOT) if f < 0 else (banks[3 - f % 2], P)
                for k in range(KC):
                    for i, (lw, lh) in enumerate(((0, 0), (0, 1), (1, 0))):
                        w = WQT[:, lw, k, :] if f < 0 else WT[:, f, lw, k, :]
                        last = nc.tensor.matmul(bank[0:m, 0:TG * P], w, hT[:, q, lh, k, :],
                                                start=k == 0 and i == 0, stop=k == KC - 1 and i == 2)
                    if k % 4 == 3 and k // 4 < len(quads):
                        turn_h(n + 1, quads[k // 4], settled)
                last.then_inc(q_ready if f < 0 else u_ready, 1)

            def slot_scores(n, q, t):
                for r in range(2):
                    last = nc.tensor.matmul(banks[4 + r], qT[0:BOT + 1, q, t * P:(t + 1) * P],
                                            s65[0:BOT + 1, r * NSLOT:(r + 1) * NSLOT], start=True, stop=True)
                last.then_inc(sc_ready, 1)

            def learned(n, f):
                pe.wait_ge(gelu_ready, 4 * n + f + 1)
                nc.tensor.matmul(banks[7][0:1, 0:TG * P], wu2s[:, f:f + 1], gl[:, f % 2, :],
                                 start=f == 0, stop=f == 3).then_inc(lrn_ready, 1)

            def turn_weights(n):
                for t in range(TG):
                    pe.wait_ge(w_ready, TG * n + t + 1)
                    for c in range(SC):
                        last = nc.tensor.transpose(quad[6 - t][:, c, :], ew[:, t, c * P:(c + 1) * P], identf)
                    last.then_inc(wT_tr, 1)

            def learned_columns(n):
                pe.wait_ge(lrow_ready, n + 1)
                for t in range(TG):
                    last = nc.tensor.matmul(banks[7][:, 300 + t:301 + t], lrow[0:1, t * P:(t + 1) * P],
                                            onesf[0:1, 0:1], start=True, stop=True)
                last.then_inc(lcol_ready, 1)

            def low_values(n):
                pe.wait_ge(e1_ready, n + 1)
                pe.wait_ge(wT_ready, TG * n + TG)
                for c in range(SC):
                    last = nc.tensor.matmul(banks[7][:, 0:TG * P], m1[:, c, :], wTt[:, c, :], start=c == 0,
                                            stop=c == SC - 1)
                last.then_inc(low_mm, 1)

            def finish(n):
                pe.wait_ge(low_ready, n + 1)
                for i in range(4 * TG):
                    t, s = i // 4, i % 4
                    if i >= 2:
                        pe.wait_ge(fin_used, 8 * n + i)
                    for j, (ll, lw) in enumerate(((0, 0), (0, 1), (1, 0))):
                        last = nc.tensor.matmul(banks[i % 2], low[:, ll, t * P:(t + 1) * P],
                                                WVUT[:, lw, s * 512:(s + 1) * 512], start=j == 0, stop=j == 2)
                    last.then_inc(fin_ready, 1)

            def group(n, q, first, last_group):
                pe.wait_ge(ht_ready, 8 * n + 8)
                if not first:
                    pe.wait_ge(gelu_ready, 4 * n)
                project(n, q, -1)
                if not first:
                    learned(n - 1, 3)
                    turn_weights(n - 1)
                    pe.wait_ge(wT_ready, TG * n)
                    pe.wait_ge(sc_used, TG * n)
                pe.wait_ge(qT_ready, n + 1)
                slot_scores(n, q, 0)
                if not first:
                    learned_columns(n - 1)
                project(n, q, 0)
                if not first:
                    low_values(n - 1)
                    finish(n - 1)
                project(n, q, 1, () if last_group else range(0, 4), not first)
                learned(n, 0)
                pe.wait_ge(sc_used, TG * n + 1)
                slot_scores(n, q, 1)
                pe.wait_ge(gelu_ready, 4 * n + 1)
                project(n, q, 2, () if last_group else range(4, 8))
                learned(n, 1)
                project(n, q, 3)
                learned(n, 2)

            for g in range(8):
                turn_h(0, g)
            pe.wait_ge(lsum_ready, 1)
            pe.wait_ge(mm_used, 32 * B + 1)
            nc.tensor.matmul(banks[7][:, 0:1], onesf, lsum, start=True, stop=True).then_inc(lsum_all, 1)
            pe.wait_ge(w3_loaded, 16 * 4)
            group(0, 0, True, False)
            with pe.Fori(0, NG // 2 - 1) as i:
                group(2 * i + 1, 1, False, False)
                group(2 * i + 2, 0, False, False)
            group(NG - 1, 1, False, True)
            learned(NG - 1, 3)
            turn_weights(NG - 1)
            learned_columns(NG - 1)
            low_values(NG - 1)
            finish(NG - 1)

        @block.vector
        def _(dve):
            order = Order(dve, dve_order)
            link, did = order.link, order.did
            tt, ts, stt = nc.vector.tensor_tensor, nc.vector.tensor_scalar, nc.vector.scalar_tensor_tensor

            for told in (kt_ready, v_ready, x1_ready, x2_ready, mm_used, attn_ready, cb_ready, rows_used, fin_used,
                         x2_counted):
                dve.sem_inc(told, 1)

            nc.vector.memset(ones16, 1.0).then_inc(consts_cast, 1)
            nc.vector.memset(onesb, 1.0).then_inc(consts_cast, 1)
            did(nc.vector.memset(mx3, 0.0))
            dve.wait_ge(consts_made, 3)
            nc.vector.tensor_copy(ident16, identf).then_inc(consts_cast, 1)
            nc.vector.tensor_copy(identb, identf).then_inc(consts_cast, 1)

            dve.wait_ge(small_in, 16 * N_SMALL)
            did(nc.vector.reciprocal(R1S, S1))
            did(nc.vector.reciprocal(R2S, S2))
            did(tt(S12, S1, S2, ALU.mult))
            did(ts(ND1, Z1, -1.0, QMID, ALU.mult, ALU.add))
            did(ts(ND2, Z2, -1.0, QMID, ALU.mult, ALU.add))
            did(ts(hbu2, hbu2, 0.5, None, ALU.mult))
            order.wait()
            did(stt(KDD, ND1, float(D), ND2, ALU.mult, ALU.mult))

            nc.vector.tensor_reduce(part, bqk, AX.X, ALU.add, apply_absolute_value=True).then_inc(bv_part, 1)
            for h in range(H):
                did(nc.vector.tensor_reduce(alpha[:, 2, h:h + 1], vb[:, h, :], AX.X, ALU.add,
                                            apply_absolute_value=True))
            did(ts(sgn, bqk, 0.0, 2.0, ALU.is_ge, ALU.mult))
            order.wait()
            did(ts(sgn, sgn, -1.0, None, ALU.add))
            link(ts(alpha[:, 2, :], alpha[:, 2, :], 1.0 / HD, None, ALU.mult))
            dve.wait_ge(bv_sum, 1)
            link(ts(alpha[:, 0:2, :], banks[7][:, 0:2 * H].rearrange("p (k h) -> p k h", h=H), 1.0 / HD, None, ALU.mult))
            for k in range(2):
                for h in range(H):
                    did(ts(btm[:, k, h, :], sgn[:, k, h, :], alpha[:, k, h:h + 1], None, ALU.mult))
            order.wait()
            link(tt(bnd, btm, bqk, ALU.subtract))
            link(tt(bnd, bnd, bqk, ALU.add))
            link(ts(part, alpha[:, 0:2, :], 1e-37, None, ALU.max))
            link(nc.vector.reciprocal(part, part))
            for k in range(2):
                for h in range(H):
                    did(ts(bnd[:, k, h, :], bnd[:, k, h, :], part[:, k, h:h + 1], None, ALU.mult))
            order.wait()
            did(tt(rse[:, 0], bnd[:, 0], bnd[:, 1], ALU.mult))
            link(tt(rse[:, 1], sgn[:, 0], sgn[:, 1], ALU.mult))
            did(tt(rse[:, 2], rse[:, 0], rse[:, 1], ALU.subtract))
            link(tt(sigscale, alpha[:, 0, :], alpha[:, 1, :], ALU.mult))
            link(ts(sigscale, sigscale, 4.0 * HD ** -0.5, None, ALU.mult))
            for h in range(H):
                hard = otmp[:, 0, :]
                link(ts(hard, vb[:, h, :], 0.0, 2.0, ALU.is_ge, ALU.mult))
                link(ts(hard, hard, -1.0, alpha[:, 2, h:h + 1], ALU.add, ALU.mult))
                link(tt(hard, hard, vb[:, h, :], ALU.subtract))
                link(tt(vb[:, h, :], hard, vb[:, h, :], ALU.add))
                link(ts(vb[:, h, :], vb[:, h, :], 1.0 / FP16_LIFT, None, ALU.mult))

            for f in range(4):
                dve.wait_ge(wu_ld[f], 16)
                did(nc.vector.tensor_reduce(mx[:, f:f + 1], wu_in[:, f, :], AX.X, ALU.max, apply_absolute_value=True))
            dve.wait_ge(wq_ld, 16)
            did(nc.vector.tensor_reduce(mx3[0:BOT, 1:2], wq_in[0:BOT, :], AX.X, ALU.max, apply_absolute_value=True))
            dve.wait_ge(wvu_ld, 16)
            did(nc.vector.tensor_reduce(mx3[:, 2:3], wvu_in.rearrange("p k v -> p (k v)"), AX.X, ALU.max,
                                        apply_absolute_value=True))
            order.wait()
            nc.vector.tensor_reduce(mx3[:, 0:1], mx[:, 0:4], AX.X, ALU.max).then_inc(abs_done, 1)

            def powers(a, z, n):
                dve.wait_ge(absmax_all, n)
                bits = lambda v: v[:, a:z].bitcast(U32)
                link(ts(bits(pw3), bits(gm3), 0x7F800000, None, ALU.bitwise_and))
                link(ts(pw3[:, a:z], pw3[:, a:z], 2.0 ** -100, None, ALU.max))
                did(ts(uns3[:, a:z], pw3[:, a:z], 1.0 / FP16_LIFT, None, ALU.mult))
                link(nc.vector.reciprocal(scl3[:, a:z], pw3[:, a:z]))

            powers(0, 3, 1)
            ts(scl3[:, 0:3], scl3[:, 0:3], FP16_LIFT, None, ALU.mult).then_inc(scales_ready, 1)
            dve.wait_ge(scales_ready, 1)
            for blk in range(11):
                for i in range(4):
                    q = 4 * blk + i
                    if blk < 6:
                        w = BOT if blk == 4 else P
                        kind = 0 if blk < 4 else blk - 3
                        lo, hi = [split[:, blk % 2, l].rearrange("p (k n) -> p k n", k=KC)[:, 4 * i:4 * i + 4, 0:w]
                                  for l in (1, 0)]
                        dve.wait_ge(quad_hi, q + 1)
                        stt(lo, quad[q % 4][:, :, 0:w], scl3[:, kind:kind + 1], hi, ALU.mult, ALU.subtract)\
                            .then_inc(quad_used, 1)
                    else:
                        dst = wvdT if blk == 6 else avT[:, blk - 7]
                        dve.wait_ge(quad_ready, q + 1)
                        nc.vector.tensor_copy(dst[:, 4 * i:4 * i + 4, :], quad[q % 4]).then_inc(quad_used, 1)
            dve.wait_ge(ak_tr, 1)
            nc.vector.tensor_copy(akT[0:BOT, :], banks[5][0:BOT, :]).then_inc(ak_copied, 1)
            nc.vector.tensor_copy(wrT[0:BOT, :], banks[4][0:BOT, 0:RDIM]).then_inc(ak_copied, 1)
            ts(s65p[0:BOT, NSLOT:], banks[5][0:BOT, :], BOT ** -0.5, None, ALU.mult).then_inc(s65_made, 1)
            dve.wait_ge(rk_ready, 1)
            nc.vector.tensor_copy(rkT[0:RDIM, :], banks[6][0:RDIM, :]).then_inc(rk_copied, 1)
            dve.wait_ge(m2_ready, 1)
            ts(s65p[0:BOT, 0:NSLOT], banks[7][0:BOT, :], RDIM ** -0.5, None, ALU.mult).then_inc(s65_made, 1)
            for s in range(SC):
                dve.wait_ge(m1_ready, s + 1)
                did(nc.vector.tensor_reduce(mx[:, 4 + s:5 + s], banks[4 + s][:, 0:VB], AX.X, ALU.max,
                                            apply_absolute_value=True))
            order.wait()
            nc.vector.tensor_reduce(mx3[:, 3:4], mx[:, 4:8], AX.X, ALU.max).then_inc(abs_done, 1)
            powers(3, 4, 2)
            for s in range(SC):
                did(ts(m1[:, s, :], banks[4 + s][:, 0:VB], scl3[:, 3:4], None, ALU.mult))
            link(tt(gsc, uns3[:, 2:3], uns3[:, 3:4], ALU.mult))
            dve.wait_ge(s65_stored, 16)
            for q in range(2):
                dve.wait_ge(split_stored[q], 16 * 3)
            dve.wait_ge(prep_done, 16 * 4)
            dve.wait_ge(wq_stored, 16)
            dve.wait_ge(abs_done, 2)

            order.start()
            with dve.Fori(0, B) as b:
                order.enter(b, DVE_BATCH)

                def stats(t, told=None):
                    for s in range(4):
                        ins = nc.vector.bn_stats(bn[:, t, s, :], X[:, t, s * 512:(s + 1) * 512])
                        if told is None or s < 3:
                            at = did(ins)
                    if told is not None:
                        ins.then_inc(told, 1)
                    return at

                def inv_dev(k, a, n, at):
                    order.wait(at)
                    for t in range(a, a + n):
                        if t == a:
                            nc.vector.memset(pause, 0)
                        did(nc.vector.bn_aggr(mv[:, t, :], bn[:, t].rearrange("p s k -> p (s k)")))
                    order.wait()
                    ts(veps[:, 0:n], mv[:, a:a + n, 1], EPS, None, ALU.add).then_inc(veps_ready, 1)
                    dve.wait_ge(sdev_ready, 5 * b + k + 1)
                    y, w = rstd[:, a:a + n], nwt[:, 0:n]
                    link(nc.vector.reciprocal(y, sdev[:, 0:n]))
                    link(tt(w, y, y, ALU.mult))
                    link(tt(w, w, veps[:, 0:n], ALU.mult))
                    link(ts(w, w, -0.5, 1.5, ALU.mult, ALU.add))
                    link(tt(y, y, w, ALU.mult))

                def normal(h, t):
                    if t < 2:
                        dve.wait_ge(kt_ready, 16 * b + 4 * h + 1)
                        dve.wait_ge(v_ready, 32 * b + 8 * h + 1)
                    else:
                        dve.wait_ge(v_ready, 32 * b + 8 * h + t )
                    ts(xn[:, t % 2, :], X[:, t, h * HD:(h + 1) * HD], mv1[:, t, 0:1], rstd1[:, t:t + 1], ALU.subtract,
                       ALU.mult).then_inc(xn_ready, 1)

                def value_low(h, t):
                    dve.wait_ge(vhi_ready, 32 * b + 8 * h + t + 1)
                    tt(V[:, h % 2, t, 1, :], xn[:, t % 2, :], V[:, h % 2, t, 0, :], ALU.subtract).then_inc(v_ready, 1)

                def keys(h, c):
                    r, sg, se = [rse[:, i, h, c:c + 1] for i in range(3)]
                    dve.wait_ge(tr_ready, 16 * b + 4 * h + c + 1)
                    lo = did(nc.vector.tensor_copy(QT[:, 1, c, :], TPL[c % 2]))
                    dve.wait_ge(qhi_ready, 16 * b + 4 * h + c + 1)
                    did(ts(KT[:, 0, c, :], QT[:, 0, c, :], sg, None, ALU.mult))
                    order.wait(lo)
                    if c < 2:
                        dve.wait_ge(v_ready, 32 * b + 8 * h + 8 + 1)
                    else:
                        dve.wait_ge(kt_ready, 16 * b + 4 * h + c )
                    link(ts(ktmp[:, c % 2, :], QT[:, 1, c, :], r, None, ALU.mult))
                    stt(KT[:, 1, c, :], QT[:, 0, c, :], se, ktmp[:, c % 2, :], ALU.mult, ALU.add)\
                        .then_inc(kt_ready, 1)

                def weights(h, s):
                    for i, k in enumerate(PC_OF[s]):
                        _, _, n, at = PIECES[k]
                        w = sig[:, k % 3, 0:n]
                        dve.wait_ge(sig_ready, 48 * b + NPC * h + k + 1)
                        if i == 0:
                            link(tt(w[:, 0:P], w[:, 0:P], mask, ALU.mult))
                        link(ts(A[:, 0, at:at + n], w, FP16_LIFT, None, ALU.mult))
                        stt(A[:, 1, at:at + n], w, FP16_LIFT, A[:, 0, at:at + n], ALU.mult, ALU.subtract)\
                            .then_inc(attn_ready, 1)

                def attended(h, t):
                    n = 32 * b + 8 * h + t + 1
                    dve.wait_ge(out_ready, n)
                    dve.wait_ge(x1_ready, (32 * b if h == 0 and t < 2 else n - 2) + 1)
                    tt(otmp[:, t % 2, :], PO[t % 2], vb[:, h, :], ALU.mult).then_inc(out_used, 1)
                    dve.wait_ge(out_used, n)
                    xs = X[:, t, h * HD:(h + 1) * HD]
                    tt(xs, xs, otmp[:, t % 2, :], ALU.add).then_inc(x1_ready, 1)

                def quant_ctx(s, j):
                    n = 16 * b + 4 * s + j + 1
                    dve.wait_ge(ctx_scaled, n)
                    if j == 0 and s >= 2:
                        dve.wait_ge(mm_ready, 32 * b + 8 * (s - 1))
                    dst = Q2[:, s % 2, 4 * j:4 * j + 4, :].rearrange("p k n -> p (k n)")
                    ts(dst, raw[:, j % 2].rearrange("p k n -> p (k n)"), MAGIC, MAGIC + QMID, ALU.add, ALU.subtract)\
                        .then_inc(raw_used, 1)
                    dve.wait_ge(raw_used, n)
                    did(ts(dst, dst, -QMID, 255.0 - QMID, ALU.max, ALU.min))

                def add_rows(s):
                    order.wait()
                    if s:
                        dve.wait_ge(cols_ready, 4 * b + s)
                    link(tt(tree[:, 0:8, :], Q2[:, s % 2, 0:8, :], Q2[:, s % 2, 8:16, :], ALU.add))
                    link(tt(tree[:, 0:4, :], tree[:, 0:4, :], tree[:, 4:8, :], ALU.add))
                    link(tt(tree[:, 0:2, :], tree[:, 0:2, :], tree[:, 2:4, :], ALU.add))
                    tt(tree[:, 0, :], tree[:, 0, :], tree[:, 1, :], ALU.add).then_inc(q2_ready, 1)

                def norm_x(t):
                    ts(xq[:, t % 2, :], X[:, t, :], mv[:, t, 0:1], rstd[:, t:t + 1], ALU.subtract, ALU.mult)\
                        .then_inc(xq_ready, 1)

                def quant_x(t):
                    dve.wait_ge(xqz_ready, 8 * b + t + 1)
                    if t >= 2:
                        dve.wait_ge(q1tr_ready, 8 * b + t - 1)
                    link(ts(q1b[:, t % 2, :], xq[:, t % 2, :], MAGIC, MAGIC + QMID, ALU.add, ALU.subtract))
                    ts(q1b[:, t % 2, :], q1b[:, t % 2, :], -QMID, 255.0 - QMID, ALU.max, ALU.min).then_inc(q1_ready, 1)

                def half_x(t):
                    dve.wait_ge(q1tr_ready, 8 * b + t + 1)
                    nc.vector.tensor_copy(q1T[:, t, 8:16, :], TQ[t % 2][1]).then_inc(q1td_ready, 1)

                def row_term(t):
                    dve.wait_ge(rows_ready, 8 * b + t + 1)
                    ts(cvec[:, t:t + 1], PO[0][:, t:t + 1], ND2, KDD, ALU.mult, ALU.add).then_inc(rows_used, 1)
                    dve.wait_ge(rows_used, 8 * b + t + 2)

                def col_term(s):
                    dve.wait_ge(cols_ready, 4 * b + s + 1)
                    if s < 2:
                        dve.wait_ge(x1_ready, 32 * b + 32 + 1)
                    else:
                        dve.wait_ge(mm_used, 32 * b + 8 * (s - 1) + 1)
                    ts(cb[:, s % 2, :], PO[1], ND1, None, ALU.mult).then_inc(cb_ready, 1)
                    dve.wait_ge(cb_ready, 4 * b + s + 2)

                def crossed(s, t):
                    n = 32 * b + 8 * s + t + 1
                    dve.wait_ge(mm_ready, n)
                    dve.wait_ge(x2_ready, (32 * b if s == 0 and t < 2 else n - 2) + 1)
                    stt(xn[:, t % 2, :], SB[t % 2], cvec[:, t:t + 1], cb[:, s % 2, :], ALU.add, ALU.add)\
                        .then_inc(mm_used, 1)
                    dve.wait_ge(mm_used, n + 1)
                    xs = X[:, t, s * 512:(s + 1) * 512]
                    stt(xs, xn[:, t % 2, :], S12, xs, ALU.mult, ALU.add).then_inc(x2_ready, 1)

                mv1, rstd1 = mv1_t, rstd1_t
                at = None
                for g in range(2):
                    for t in range(4 * g, 4 * g + 4):
                        dve.wait_ge(x_loaded[t], 16 * b + 16)
                        at = stats(t)
                    inv_dev(g, 4 * g, 4, at)
                did(nc.vector.tensor_copy(mv1, mv))
                link(nc.vector.tensor_copy(rstd1, rstd))
                for t in range(NT + 1):
                    if t < NT:
                        normal(0, t)
                    if t:
                        value_low(0, t - 1)
                for c in range(DC):
                    keys(0, c)
                for h in range(H):
                    last = h == H - 1
                    for s in range(NT):
                        weights(h, s)
                        if s >= 3:
                            attended(h, s - 3)
                            if last:
                                dve.wait_ge(x1_ready, 32 * b + 8 * h + s - 1)
                                at = stats(s - 3)
                        if not last:
                            for t in V_AFTER[s]:
                                normal(h + 1, t)
                            for t in V_AFTER[s]:
                                value_low(h + 1, t)
                        elif s in CTX_AFTER:
                            quant_ctx(0, CTX_AFTER[s])
                    if not last:
                        attended(h, 5)
                        keys(h + 1, 0)
                        keys(h + 1, 1)
                        attended(h, 6)
                        keys(h + 1, 2)
                        keys(h + 1, 3)
                        attended(h, 7)
                    else:
                        add_rows(0)
                        attended(h, 5)
                        dve.wait_ge(x1_ready, 32 * b + 8 * h + 6 + 1)
                        stats(5)
                        inv_dev(2, 0, 4, at)
                        norm_x(0)
                        norm_x(1)
                        for t in (6, 7):
                            attended(h, t)
                            dve.wait_ge(x1_ready, 32 * b + 8 * h + t + 2)
                            at = stats(t)
                        inv_dev(3, 4, 4, at)
                for t in range(NT + 3):
                    if t < NT:
                        quant_x(t)
                    if t + 2 < NT:
                        norm_x(t + 2)
                    if 1 <= t <= NT:
                        half_x(t - 1)
                    if t == NT:
                        for j in range(4):
                            quant_ctx(1, j)
                    if 2 <= t < NT + 2:
                        row_term(t - 2)
                    if t == 3:
                        col_term(0)
                    if 3 <= t:
                        crossed(0, t - 3)
                        if t == NT:
                            add_rows(1)
                for s in range(1, NS):
                    col_term(s)
                    for t in range(NT):
                        crossed(s, t)
                        if s < NS - 1:
                            if t < 4:
                                quant_ctx(s + 1, t)
                            if t == 5:
                                add_rows(s + 1)
                        else:
                            dve.wait_ge(x2_ready, 32 * b + 8 * s + t + 2)
                            stats(t, x2_counted)
                dve.wait_ge(x2_counted, 8 * b + 8 + 1)
                inv_dev(4, 0, NT, None)
                link(tt(vh, rstd, rstd, ALU.mult))
                link(tt(vh, vh, mv[:, :, 1], ALU.mult))
                did(nc.vector.tensor_copy(tab[:, 0, bass.ds(b * NT, NT)], mv[:, :, 0]))
                did(nc.vector.tensor_copy(tab[:, 1, bass.ds(b * NT, NT)], rstd))
                link(nc.vector.tensor_copy(tab[:, 2, bass.ds(b * NT, NT)], vh))
                nc.vector.memset(pause, 0).then_inc(tab_ready, 1)
            order.leave(B, DVE_BATCH)

            for q in range(2):
                did(nc.vector.memset(qT[BOT:BOT + 1, q, :], 1.0))
            order.start()

            def normal_h(n, q):
                dve.wait_ge(y_ready, TG * n + 1)
                dve.wait_ge(ht_tr, 8 * n + 1)
                link(nc.vector.tensor_copy(cur[:, q], tab[:, :, bass.ds(n * TG, TG)]))
                for t in range(TG):
                    dve.wait_ge(y_loaded[2 * q + t], 16 * (turn_of(n, q) + 1))
                    ts(hs[:, t, :], Y[:, q, t, :], cur[:, q, 0, t:t + 1], cur[:, q, 1, t:t + 1], ALU.subtract,
                       ALU.mult).then_inc(h_ready, 1)

            def low_h(n, q, g):
                t, k = g // 4, g % 4
                dve.wait_ge(ht_hi, 8 * n + g + 1)
                tt(hT[:, q, 1, 4 * k:4 * k + 4, t * P:(t + 1) * P], quad[g % 2],
                   hT[:, q, 0, 4 * k:4 * k + 4, t * P:(t + 1) * P], ALU.subtract).then_inc(ht_ready, 1)

            def choose(n, t):
                dve.wait_ge(sc_ready, TG * n + t + 1)
                nc.vector.memset(pause, 0)
                link(nc.vector.max(m8[:, t, :], banks[4]))
                nc.vector.memset(pause, 0)
                link(nc.vector.match_replace(rep, m8[:, t, :], banks[4], LOWEST))
                link(tt(nsel, rep, banks[4], ALU.is_equal))
                stt(am[:, t, :], nsel, FAR, banks[5], ALU.mult, ALU.add).then_inc(sc_used, 1)
                dve.wait_ge(sc_used, TG * n + t + 1)
                nc.vector.tensor_reduce(nmx[:, t:t + 1], am[:, t, :], AX.X, ALU.max, negate=True)\
                    .then_inc(nmx_ready, 1)

            def weigh(n, t):
                dve.wait_ge(e_ready, TG * n + t + 1)
                link(nc.vector.reciprocal(rden[:, t:t + 1], den[:, t:t + 1]))
                ts(ew[:, t, :], ew[:, t, :], rden[:, t:t + 1], None, ALU.mult).then_inc(w_ready, 1)

            def weights_rows(n):
                for t in range(TG):
                    dve.wait_ge(wT_tr, TG * n + t + 1)
                    nc.vector.tensor_copy(wTt[:, :, t * P:(t + 1) * P], quad[6 - t]).then_inc(wT_ready, 1)

            def gate_and_finish(n, q, more=False):
                dve.wait_ge(e1_ready, n + 1)
                link(stt(ge[:, 3, :], ge[:, 0, :], 1.25, cur[:, q, 2, :], ALU.mult, ALU.add))
                link(ts(ge[:, 3, :], ge[:, 3, :], 0.0, 5.0, ALU.max, ALU.min))
                link(ts(ge[:, 3, :], ge[:, 3, :], -0.5, 1.0 / 1.5, ALU.add, ALU.mult))
                link(ts(ge[:, 4, :], ge[:, 3, :], 0.0, 1.0, ALU.max, ALU.min))
                ts(ge[:, 5, :], ge[:, 4, :], gw[:, 0:1], gw[:, 1:2], ALU.mult, ALU.add).then_inc(z_ready, 1)
                if more:
                    normal_h(n + 2, q)
                dve.wait_ge(e2_ready, n + 1)
                dve.wait_ge(fin_used, 8 * n + 1)
                link(ts(ge[:, 8, :], ge[:, 6, :], 0.5, 0.5, ALU.mult, ALU.add))
                link(stt(ge[:, 9, :], ge[:, 8, :], 0.05, ge[:, 8, :], ALU.is_ge, ALU.mult))
                link(ts(ge[:, 9, :], ge[:, 9, :], gsc, None, ALU.mult))
                dve.wait_ge(low_hi, n + 1)
                stt(low[:, 1, :], banks[7][:, 0:TG * P], FP16_LIFT, low[:, 0, :], ALU.mult, ALU.subtract)\
                    .then_inc(low_ready, 1)
                for i in range(4 * TG):
                    t, s = i // 4, i % 4
                    if s == 0:
                        dve.wait_ge(y_ready, TG * n + t + 2)
                    dve.wait_ge(fin_ready, 8 * n + i + 1)
                    fs = F[:, q, t, s * 512:(s + 1) * 512]
                    stt(fs, banks[i % 2], ge[:, 9, t:t + 1], fs, ALU.mult, ALU.add).then_inc(fin_used, 1)

            def learned_row(n):
                dve.wait_ge(lrn_ready, 4 * n + 5)
                nc.vector.tensor_copy(lrow[0:1, :], banks[7][0:1, 0:TG * P]).then_inc(lrow_ready, 1)

            def group(n, q, first, last_group):
                if not first:
                    learned_row(n - 1)
                    weights_rows(n - 1)
                choose(n, 0)
                if not first:
                    gate_and_finish(n - 1, 1 - q, not last_group)
                elif not last_group:
                    normal_h(n + 1, 1 - q)
                if not last_group:
                    for g in range(0, 4):
                        low_h(n + 1, 1 - q, g)
                choose(n, 1)
                weigh(n, 0)
                if not last_group:
                    for g in range(4, 8):
                        low_h(n + 1, 1 - q, g)
                weigh(n, 1)

            turn = [0]

            def turn_of(n, q):
                return n // 2 if isinstance(n, int) else turn[0] + 1

            normal_h(0, 0)
            for g in range(8):
                low_h(0, 0, g)
            dve.wait_ge(log_ready, 1)
            nc.vector.tensor_reduce(lsum, logv, AX.X, ALU.add).then_inc(lsum_ready, 1)
            dve.wait_ge(lsum_all, 1)
            link(ts(lmean, banks[7][:, 0:1], 1.0 / (B * T), 1e-6, ALU.mult, ALU.add))
            link(nc.vector.reciprocal(lmean, lmean))
            link(ts(tab[:, 2, :], logv, lmean, 0.5, ALU.mult, ALU.mult))
            link(ts(tab[:, 2, :], tab[:, 2, :], 1.25, None, ALU.add))
            link(nc.vector.tensor_copy(cur[:, 0, 2, :], tab[:, 2, 0:TG]))
            group(0, 0, True, False)
            order.start()
            with dve.Fori(0, NG // 2 - 1) as i:
                order.enter(i, DVE_PAIR)
                turn[0] = i
                group(2 * i + 1, 1, False, False)
                group(2 * i + 2, 0, False, False)
            order.leave(NG // 2 - 1, DVE_PAIR)
            group(NG - 1, 1, False, True)
            learned_row(NG - 1)
            weights_rows(NG - 1)
            gate_and_finish(NG - 1, 1)


_INS = ['x', 'ctx_4096', 'L0_attn_bv_q', 'L0_attn_bv_k', 'L0_attn_bv_v', 'L0_xattn_x1_scale', 'L0_xattn_x1_zp',
        'L0_xattn_x2_scale', 'L0_xattn_x2_zp', 'L0_ffn_Wq', 'L0_ffn_Wr', 'L0_ffn_aux_keys', 'L0_ffn_aux_values',
        'L0_ffn_Wvd', 'L0_ffn_Wvu', 'L0_ffn_Wu1', 'L0_ffn_bu1', 'L0_ffn_Wu2', 'L0_ffn_bu2', 'L0_ffn_gate_w1',
        'L0_ffn_gate_bias', 'L0_ffn_log_rel']


def kernel(**inputs):
    import numpy as _np
    import concourse.bacc as _bacc
    from concourse import mybir as _mybir
    from concourse.bass_utils import run_bass_kernel_spmd as _run

    nc = _bacc.Bacc("TRN2", target_bir_lowering=False, num_devices=1)
    arrays, args = {}, []
    for name in _INS:
        a = _np.ascontiguousarray(inputs[name])
        arrays[f"in_{name}_dram"] = a
        args.append(nc.dram_tensor(f"in_{name}_dram", a.shape, _mybir.dt.from_np(a.dtype), kind="ExternalInput").ap())
    args.append(nc.dram_tensor("out_0_dram", (B, T, D), F32, kind="ExternalOutput").ap())
    nc.disable_value_cache = True
    decoder_kernel(nc, *args)
    r = _run(nc, [arrays], core_ids=[0])
    return r.results[0]["out_0_dram"]
```

```python
from contextlib import ExitStack

import concourse.bass as bass
from concourse import mybir

ALU = mybir.AluOpType
ACT = mybir.ActivationFunctionType
AX = mybir.AxisListType
F32 = mybir.dt.float32
F16 = mybir.dt.float16
BF16 = mybir.dt.bfloat16
U32 = mybir.dt.uint32

P = 128
B, T, D = 2, 1024, 2048
H = 4
HD = D // H
NT = T // P
DC = HD // P
KC = D // P
NS = D // 512
RDIM, BOT, NSLOT, VB, FU = 48, 64, 512, 128, 512
SC = NSLOT // P
EPS = 1e-5
FP16_LIFT = 4096.0
MAGIC = 1.5 * 2.0 ** 23
QMID = 128.0
RSQRT_MAGIC = float(0x5F3759DF)
LOWEST = -3.0e38
FAR = -1.0e30
TG = 2
NG = B * NT // TG

PIECES = []
_at = 0
for _s in range(NT):
    for _a, _z in ((P * _s, T // 2), (max(P * _s, T // 2), T)):
        if _a < _z:
            PIECES.append((_s, _a, _z - _a, _at))
            _at += _z - _a
ACOLS = _at
NPC = len(PIECES)
PC_UNTIL = [max(i for i, p in enumerate(PIECES) if p[0] == s) + 1 for s in range(NT)]
PC_OF = [[i for i, p in enumerate(PIECES) if p[0] == s] for s in range(NT)]
STORE = [min(p[3] for p in PIECES if p[0] == s) for s in range(NT)]

V_AFTER = [[0, 1], [2, 3], [4], [5], [6], [7], [], []]
CTX_AFTER = {1: (0, 0), 2: (0, 1), 3: (0, 2), 4: (0, 3), 5: (1, 0), 6: (1, 1)}

MOVES = [(s, 0, NT) for s in range(NS - 1)] + [(NS - 1, 0, 2 * TG), (NS - 1, 2 * TG, NT)]

W_X = 0
W_V = W_X + NT * D
W_QT = W_V + NT * 2 * HD
W_KT = W_QT + DC * T
W_A = W_KT + DC * T
W_Q2 = W_A + ACOLS
W_SIG = W_Q2 + KC * HD
W_XN = W_SIG + 3 * 512
W_OT = W_XN + 2 * 512
W_VB = W_OT + 2 * 512
W_CONST = W_VB + D
W_END = W_CONST + 1900

DVE_BATCH, DVE_PAIR = 255, 34


class Order:

    def __init__(self, eng, sem):
        self.eng, self.sem, self.total, self.base, self.n = eng, sem, 0, 0, 0

    def did(self, ins):
        ins.then_inc(self.sem, 1)
        self.n += 1
        return self.n

    def wait(self, at=None):
        self.eng.wait_ge(self.sem, self.base + (self.n if at is None else at))

    def link(self, ins):
        self.did(ins)
        self.wait()

    def enter(self, turn, per):
        self.base, self.n = self.total + turn * per, 0

    def leave(self, turns, per):
        assert self.n == per, f"count a turn: {self.n}, not {per}"
        self.total += turns * per
        self.base, self.n = self.total, 0

    def start(self):
        self.total += self.n
        self.base, self.n = self.total, 0


def decoder_kernel(nc, x, ctx, bv_q, bv_k, bv_v, s1, z1, s2, z2, wq, wr, aux_k, aux_v, wvd, wvu,
                   wu1, bu1, wu2, bu2, gate_w1, gate_bias, log_rel, out):
    x_r = x.rearrange("b (t p) d -> (b t) p d", p=P)
    out_r = out.rearrange("b (t p) d -> (b t) p d", p=P)
    ctx_r = ctx.rearrange("b (j k p) (s n) -> j s b p k n", p=P, k=4, n=512)
    x2_d = nc.dram_tensor("x2_spill", (B * NT, P, D), F32, kind="Internal").ap()
    wt_d = nc.dram_tensor("wu1_split", (P, 4, 2 * KC * P), F16, kind="Internal").ap()
    wqt_d = nc.dram_tensor("wq_split", (P, 2, KC, BOT), F16, kind="Internal").ap()
    wvut_d = nc.dram_tensor("wvu_split", (P, 2 * D), F16, kind="Internal").ap()
    s65_d = nc.dram_tensor("score_rhs", (BOT + 1, 2 * NSLOT), F32, kind="Internal").ap()

    es = ExitStack()
    with es:
        es.enter_context(nc.allow_non_contiguous_dma("small vectors are laid out by partition"))

        def sem(name):
            return es.enter_context(nc.semaphore(name))

        arena = es.enter_context(nc.sbuf_tensor("arena", [P, W_END], F32))
        banks = [es.enter_context(nc.psum_tensor(f"bank{i}", [P, 512], F32))[:, :] for i in range(8)]

        def view(word, words, dt=F32):
            ap = arena[:, word:word + words]
            return ap if dt is F32 else ap.bitcast(dt)

        free = [W_CONST]

        def small(words, dt=F32):
            free[0] += words
            assert free[0] <= W_END
            return view(free[0] - words, words, dt)

        identf, onesf, mask = small(P), small(P), small(P)
        ident16, identb = small(P // 2, F16), small(P // 2, BF16)
        ones16, onesb = small(P // 2, F16), small(1, BF16)
        mask16 = small(P // 2, F16)
        m1 = small(SC * VB).rearrange("p (c v) -> p c v", c=SC)
        qp = small(10)
        S1, Z1, S2, Z2, R1S, R2S, S12, ND2, ND1, KDD = [qp[:, i:i + 1] for i in range(10)]
        alpha = small(4 * H).rearrange("p (k h) -> p k h", h=H)
        part = small(2 * H).rearrange("p (k h) -> p k h", h=H)
        bqk = small(2 * H * DC).rearrange("p (k h c) -> p k h c", k=2, h=H)
        sgn = small(2 * H * DC).rearrange("p (k h c) -> p k h c", k=2, h=H)
        btm = small(2 * H * DC).rearrange("p (k h c) -> p k h c", k=2, h=H)
        bnd = small(2 * H * DC).rearrange("p (k h c) -> p k h c", k=2, h=H)
        rse = small(3 * H * DC).rearrange("p (k h c) -> p k h c", k=3, h=H)
        sigscale = small(H)
        mx = small(8)
        mx3, gm3, pw3, scl3, uns3 = small(4), small(4), small(4), small(4), small(4)
        bn = small(NT * 4 * 6).rearrange("p (t s k) -> p t s k", t=NT, s=4)
        mv = small(NT * 2).rearrange("p (t k) -> p t k", k=2)
        rstd, veps, nwt = small(NT), small(NT), small(NT)
        xscale, xbias, bias1 = small(NT), small(NT), small(NT)
        vh = small(NT)
        rstd1 = small(NT)
        cvec = small(NT)
        tab = small(3 * B * NT).rearrange("p (k t) -> p k t", k=3)
        logv, lsum, lmean = small(B * NT), small(1), small(1)
        bu1s, wu2s, hbu2, gw = small(4), small(4), small(1), small(2)
        gsc = small(1)
        cur = small(2 * 3 * TG).rearrange("p (q k t) -> p q k t", q=2, k=3)
        m8 = small(2 * 8).rearrange("p (t k) -> p t k", k=8)
        nmx, den, rden = small(2), small(2), small(2)
        ge = small(10 * TG).rearrange("p (k t) -> p k t", t=TG)
        pause = small(1, U32)

        X = view(W_X, NT * D).rearrange("p (t d) -> p t d", t=NT)
        V = view(W_V, NT * 2 * HD, F16).rearrange("p (q t l d) -> p q t l d", q=2, t=NT, l=2)
        QT = view(W_QT, DC * T, F16).rearrange("p (l c t) -> p l c t", l=2, c=DC)
        KT = view(W_KT, DC * T, F16).rearrange("p (l c t) -> p l c t", l=2, c=DC)
        A = view(W_A, ACOLS, F16).rearrange("p (l t) -> p l t", l=2)
        sig = view(W_SIG, 3 * 512).rearrange("p (q n) -> p q n", q=3)
        xn = view(W_XN, 2 * 512).rearrange("p (q n) -> p q n", q=2)
        ktmp = view(W_XN, 2 * 512, F16).rearrange("p (q n) -> p q n", q=2)
        otmp = view(W_OT, 2 * 512).rearrange("p (q n) -> p q n", q=2)
        vb = view(W_VB, D).rearrange("p (h d) -> p h d", h=H)
        Q2 = view(W_Q2, KC * HD, BF16).rearrange("p (q k n) -> p q k n", q=2, k=KC)
        xq = [view(W_Q2 + KC * HD // 2 + D, D), view(W_SIG, D)] + [view(W_V + (2 + t % 2) * D, D) for t in range(2, NT)]
        q1b = view(W_QT + DC * T // 2, D, BF16).rearrange("p (q d) -> p q d", q=2)
        tree = view(W_QT, DC * T // 2, F16).rearrange("p (k n) -> p k n", n=512)
        raw = view(W_V, 2 * D).rearrange("p (q k n) -> p q k n", q=2, k=4)
        q1T = view(W_KT, NT * D // 2, BF16).rearrange("p (t k n) -> p t k n", t=NT, k=KC)
        cb = otmp

        wu_in = [view(w, D) for w in (W_V, W_V + D, W_KT, W_KT + D)]
        wq_in = view(W_QT, D)
        wvu_in = view(W_QT + D, D).rearrange("p (k v) -> p k v", v=VB)
        wvd_in = view(W_V + 2 * D, D)
        wvdT = view(W_V + 3 * D, D).rearrange("p (k v) -> p k v", v=VB)
        split = view(W_A, 6 * D, F16).rearrange("p (q l d) -> p q l d", q=6, l=2)
        av_in = wu_in
        avT = [view(W_A + i * D, D).rearrange("p (k n) -> p k n", k=KC) for i in range(4)]
        s65p = view(W_SIG, 2 * NSLOT)
        ak_in = view(W_SIG + 1024, SC * BOT).rearrange("p (c d) -> p c d", c=SC)
        akT = view(W_SIG + 1280, NSLOT)
        rkT = view(W_SIG + 1792, NSLOT)
        wr_in, wrT = view(W_SIG + 2304, BOT), view(W_SIG + 2368, RDIM)

        Y = view(0, 2 * TG * D).rearrange("p (q t d) -> p q t d", q=2, t=TG)
        hT = view(4 * D, 4 * D, F16).rearrange("p (q l k t) -> p q l k t", q=2, l=2, k=KC)
        WT = view(W_V, 4 * D, F16).rearrange("p (f l k n) -> p f l k n", f=4, l=2, k=KC)
        WQT = view(W_QT, KC * BOT, F16).rearrange("p (l k n) -> p l k n", l=2, k=KC)
        WVUT = view(W_QT + KC * BOT, D, F16).rearrange("p (l d) -> p l d", l=2)
        s65 = view(W_QT + KC * BOT + D, 2 * NSLOT)
        hs = view(W_KT, TG * D).rearrange("p (t d) -> p t d", t=TG)
        w0 = W_KT + TG * D
        gl = view(w0, 512).rearrange("p (q t) -> p q t", q=2)
        qT = view(w0 + 512, 512).rearrange("p (q t) -> p q t", q=2)
        rep = view(w0 + 1024, 512)
        am = view(w0 + 1536, 1024).rearrange("p (t n) -> p t n", t=2)
        ew = view(w0 + 2560, 1024).rearrange("p (t n) -> p t n", t=2)
        nsel = view(w0 + 3584, 512)
        wTt = view(w0 + 4096, 1024).rearrange("p (c t) -> p c t", c=SC)
        low = view(w0 + 5120, 256, F16).rearrange("p (l t) -> p l t", l=2)
        lrow = view(w0 + 5376, 256)
        F = view(w0 + 5632, 2 * TG * D).rearrange("p (q t d) -> p q t d", q=2, t=TG)

        TPH = [banks[0][:, :].bitcast(F16), banks[2][:, :].bitcast(F16)]
        TPL = [banks[1][:, :].bitcast(F16), banks[3][:, :].bitcast(F16)]
        TQ = [[banks[2 * i + j][:, :].bitcast(BF16).rearrange("p (k n) -> p k n", k=8) for j in range(2)]
              for i in range(2)]
        SB = [banks[4], banks[5]]
        PO = [banks[6], banks[7]]
        quad = [banks[i][:, :].rearrange("p (k n) -> p k n", k=4) for i in range(8)]

        wT_bank = [quad[6], quad[1]]
        fin_bank = [banks[4], banks[5], banks[0], banks[1]]

        consts_made = sem("consts_made")
        consts_cast = sem("consts_cast")
        small_in, gates_in = sem("small_in"), sem("gates_in")
        wu_ld = [sem(f"wu_ld{i}") for i in range(4)]
        wq_ld, wvu_ld, wvd_ld = sem("wq_ld"), sem("wvu_ld"), sem("wvd_ld")
        av_ld = [sem(f"av_ld{i}") for i in range(4)]
        abs_done, absmax_all = sem("abs_done"), sem("absmax_all")
        quad_copied, m1_copied, bv_read = sem("quad_copied"), sem("m1_copied"), sem("bv_read")
        scales_ready = sem("scales_ready")
        quad_ready, quad_hi, quad_used = sem("quad_ready"), sem("quad_hi"), sem("quad_used")
        split_stored = [sem(f"split_stored{i}") for i in range(6)]
        bv_part, bv_sum = sem("bv_part"), sem("bv_sum")
        alpha_ready, vb_ready = sem("alpha_ready"), sem("vb_ready")
        ak_tr, ak_copied, rk_ready, rk_copied, m2_ready = (sem("ak_tr"), sem("ak_copied"), sem("rk_ready"),
                                                           sem("rk_copied"), sem("m2_ready"))
        s65_made, s65_row, s65_stored = sem("s65_made"), sem("s65_row"), sem("s65_stored")
        m1_ready = sem("m1_ready")
        prep_done = sem("prep_done")

        x_loaded = [sem(f"x_loaded{i}") for i in range(len(MOVES))]
        ctx_loaded = [sem(f"ctx_loaded{q}") for q in range(2)]
        x2_stored = [sem(f"x2_stored{i}") for i in range(len(MOVES))]
        norm_ready = sem("norm_ready")
        xn_ready, vhi_ready, v_ready = sem("xn_ready"), sem("vhi_ready"), sem("v_ready")
        tr_ready, qhi_ready, qlo_ready, kt_ready = sem("tr_ready"), sem("qhi_ready"), sem("qlo_ready"), sem("kt_ready")
        scores_ready, sig_ready, attn_ready = sem("scores_ready"), sem("sig_ready"), sem("attn_ready")
        ahi_ready = sem("ahi_ready")
        out_ready, out_used, x1_ready = sem("out_ready"), sem("out_used"), sem("x1_ready")
        affine_ready, xq_ready, q1_ready = sem("affine_ready"), sem("xq_ready"), sem("q1_ready")
        q1tr_ready, q1t_ready, rows_ready = sem("q1tr_ready"), sem("q1t_ready"), sem("rows_ready")
        ctx_scaled, raw_used, q2_ready = sem("ctx_scaled"), sem("raw_used"), sem("q2_ready")
        cols_ready, cb_ready, rows_used = sem("cols_ready"), sem("cb_ready"), sem("rows_used")
        mm_ready, mm_used, x2_ready, x2_counted = sem("mm_ready"), sem("mm_used"), sem("x2_ready"), sem("x2_counted")

        w3_loaded = sem("w3_loaded")
        tab_ready, log_ready, lsum_ready, lsum_all = sem("tab_ready"), sem("log_ready"), sem("lsum_ready"), sem("lsum_all")
        y_loaded = [sem(f"y_loaded{q}") for q in range(4)]
        h_ready, y_ready = sem("h_ready"), sem("y_ready")
        ht_tr, ht_hi, ht_ready = sem("ht_tr"), sem("ht_hi"), sem("ht_ready")
        q_ready, qT_ready, sc_ready, sc_used = sem("q_ready"), sem("qT_ready"), sem("sc_ready"), sem("sc_used")
        nmx_ready, e_ready, w_ready = sem("nmx_ready"), sem("e_ready"), sem("w_ready")
        u_ready, gelu_ready, lrn_ready, lrow_ready, lcol_ready = (sem("u_ready"), sem("gelu_ready"), sem("lrn_ready"),
                                                                  sem("lrow_ready"), sem("lcol_ready"))
        e1_ready, z_ready, e2_ready = sem("e1_ready"), sem("z_ready"), sem("e2_ready")
        wT_tr, wT_ready, low_mm, low_hi, low_ready = (sem("wT_tr"), sem("wT_ready"), sem("low_mm"), sem("low_hi"),
                                                      sem("low_ready"))
        fin_ready, fin_used = sem("fin_ready"), sem("fin_used")
        stored = [sem(f"stored{q}") for q in range(4)]
        dve_order, pool_order = sem("dve_order"), sem("pool_order")

        N_SMALL = 16

        block = es.enter_context(nc.Block())


        @block.sync
        def _(sp):
            for i in range(len(MOVES)):
                sp.sem_inc(x2_stored[i], 1)
            for q in range(4):
                sp.sem_inc(stored[q], 1)
            for f in range(4):
                sp.dma_start(wu_in[f], wu1[f * P:(f + 1) * P, :]).then_inc(wu_ld[f], 16)
            sp.dma_start(wq_in[0:BOT, :], wq).then_inc(wq_ld, 16)
            sp.dma_start(wvu_in, wvu.rearrange("(k p) v -> p k v", p=P)).then_inc(wvu_ld, 16)
            with sp.Fori(0, B) as b:
                for i, (s, a, z) in enumerate(MOVES):
                    sp.wait_ge(x2_stored[i], 16 * b + 1)
                    sp.dma_start(X[:, a:z, s * 512:(s + 1) * 512],
                                 x_r[bass.ds(b * NT + a, z - a), :, s * 512:(s + 1) * 512]
                                 .rearrange("t p n -> p t n")).then_inc(x_loaded[i], 16)
                sp.wait_ge(out_ready, 32 * b + 24)
                for s in range(NS):
                    for j in range(4):
                        if s or j >= 2:
                            sp.wait_ge(raw_used, 16 * b + 4 * s + j - 1)
                        sp.dma_start(raw[:, j % 2],
                                     ctx_r[j, s, bass.ds(b, 1)].rearrange("a p k n -> p (a k) n"))\
                          .then_inc(ctx_loaded[j % 2], 16)

            def store(n, q):
                for t in range(TG):
                    sp.wait_ge(fin_used, 8 * n + 4 * t + 5)
                    sp.dma_start(out_r[bass.ds(n * TG + t, 1)].rearrange("a p d -> p (a d)"), F[:, q, t, :])\
                      .then_inc(stored[2 * q + t], 16)

            with sp.Fori(0, NG // 2) as i:
                for q in range(2):
                    store(2 * i + q, q)
            for q in range(4):
                sp.wait_ge(stored[q], 16 * (NG // 2) + 1)

        @block.gpsimd
        def _(pool):
            order = Order(pool, pool_order)
            pool.sem_inc(y_ready, 1)
            pool.memset(onesf, 1.0).then_inc(consts_made, 1)
            order.did(pool.memset(identf, 0.0))
            order.did(pool.memset(mask, 1.0))
            order.wait()
            pool.affine_select(out=identf, in_=identf, compare_op=ALU.not_equal, fill=1.0, base=0,
                               pattern=[[-1, P]], channel_multiplier=1).then_inc(consts_made, 1)
            pool.affine_select(out=mask, in_=mask, compare_op=ALU.is_ge, fill=0.0, base=0,
                               pattern=[[1, P]], channel_multiplier=-1).then_inc(consts_made, 1)
            pool.wait_ge(abs_done, 1)
            pool.partition_all_reduce(gm3[:, 0:3], mx3[:, 0:3], P, bass.bass_isa.ReduceOp.max)\
                .then_inc(absmax_all, 1)
            pool.wait_ge(s65_made, 2)
            pool.wait_ge(s65_row, 32)
            pool.dma_start(s65_d, s65p[0:BOT + 1, :]).then_inc(s65_stored, 16)
            for blk in range(6):
                pool.wait_ge(quad_used, 4 * blk + 4)
                src = split[:, blk]
                if blk < 4:
                    dst, src = wt_d[:, blk, :], src.rearrange("p l d -> p (l d)")
                elif blk == 4:
                    dst = wqt_d
                    src = src.rearrange("p l (k n) -> p l k n", k=KC)[:, :, :, 0:BOT]
                else:
                    dst, src = wvut_d, src.rearrange("p l d -> p (l d)")
                if blk == 4:
                    for l in range(2):
                        pool.dma_start(dst[:, l], src[:, l]).then_inc(split_stored[blk], 16)
                else:
                    pool.dma_start(dst, src).then_inc(split_stored[blk], 16)
                if blk < SC:
                    pool.dma_start(av_in[blk], aux_v[blk * P:(blk + 1) * P, :]).then_inc(av_ld[blk], 16)

            pool.wait_ge(alpha_ready, 1)
            hard = otmp[:, 0, :]
            for h in range(H):
                order.link(pool.tensor_scalar(hard, vb[:, h, :], 0.0, 2.0, ALU.is_ge, ALU.mult))
                order.link(pool.tensor_scalar(hard, hard, -1.0, alpha[:, 2, h:h + 1], ALU.add, ALU.mult))
                order.link(pool.tensor_tensor(hard, hard, vb[:, h, :], ALU.subtract))
                order.link(pool.tensor_tensor(vb[:, h, :], hard, vb[:, h, :], ALU.add))
                pool.tensor_scalar(vb[:, h, :], vb[:, h, :], 1.0 / FP16_LIFT, None, ALU.mult).then_inc(vb_ready, 1)

            pool.wait_ge(raw_used, 16 * B)
            pool.wait_ge(cols_ready, NS * B)
            for blk in range(6):
                pool.wait_ge(split_stored[blk], 32 if blk == 4 else 16)
            pool.wait_ge(s65_stored, 16)
            pool.dma_start(WQT, wqt_d).then_inc(w3_loaded, 16)
            pool.dma_start(s65[0:BOT + 1, :], s65_d).then_inc(w3_loaded, 16)
            pool.dma_start(WT.rearrange("p f l k n -> p f (l k n)"), wt_d).then_inc(w3_loaded, 16)
            pool.dma_start(WVUT.rearrange("p l d -> p (l d)"), wvut_d).then_inc(w3_loaded, 16)

            def load(n, q):
                for t in range(TG):
                    pool.dma_start(Y[:, q, t, :], x2_d[bass.ds(n * TG + t, 1)].rearrange("a p d -> p (a d)"))\
                        .then_inc(y_loaded[2 * q + t], 16)

            def add_h(n, q):
                for t in range(TG):
                    pool.wait_ge(h_ready, TG * n + t + 1)
                    pool.wait_ge(stored[2 * q + t], results_out(n))
                    pool.tensor_tensor(F[:, q, t, :], Y[:, q, t, :], hs[:, t, :], ALU.add).then_inc(y_ready, 1)

            for i in range(len(MOVES) - 1):
                pool.wait_ge(x2_stored[i], 16 * B + 1)
            load(0, 0)
            load(1, 1)
            pool.wait_ge(abs_done, 2)
            pool.partition_all_reduce(gm3[:, 3:4], mx3[:, 3:4], P, bass.bass_isa.ReduceOp.max)\
                .then_inc(absmax_all, 1)
            pool.wait_ge(x2_stored[-1], 16 * B + 1)
            with pool.Fori(0, NG // 2 - 1) as i:
                for q in range(2):
                    results_out = lambda n: 16 * i + 1
                    add_h(2 * i + q, q)
                    pool.wait_ge(y_ready, 2 * TG * i + TG * q + TG + 1)
                    load(2 * i + q + 2, q)
            results_out = lambda n: 16 * (n // 2) + 1
            add_h(NG - 2, 0)
            add_h(NG - 1, 1)

        @block.scalar
        def _(act):
            for i, a in enumerate((s1, z1, s2, z2)):
                act.dma_start(qp[:, i:i + 1], a.partition_broadcast(P)).then_inc(small_in, 16)
            act.dma_start(wr_in[0:RDIM, :], wr).then_inc(prep_done, 16)
            act.dma_start(ak_in, aux_k.rearrange("(c p) d -> p c d", p=P)).then_inc(prep_done, 16)
            act.dma_start(s65p[BOT:BOT + 1, 0:NSLOT], log_rel.rearrange("(a n) -> a n", a=1)).then_inc(s65_row, 16)
            act.dma_start(s65p[BOT:BOT + 1, NSLOT:], log_rel.rearrange("(a n) -> a n", a=1)).then_inc(s65_row, 16)
            for i, h in enumerate((bv_q, bv_k)):
                for hh in range(H):
                    act.dma_start(bqk[:, i, hh, :], h[hh].rearrange("(c p) -> p c", p=P)).then_inc(small_in, 16)
            act.dma_start(vb, bv_v.partition_broadcast(P)).then_inc(small_in, 16)
            act.dma_start(bu1s, bu1.rearrange("(c p) -> p c", p=P)).then_inc(small_in, 16)
            act.dma_start(wu2s, wu2.rearrange("a (c p) -> p (a c)", p=P)).then_inc(small_in, 16)
            act.dma_start(hbu2, bu2.partition_broadcast(P)).then_inc(small_in, 16)
            act.dma_start(gw[:, 0:1], gate_w1.partition_broadcast(P)).then_inc(gates_in, 16)
            act.dma_start(gw[:, 1:2], gate_bias.partition_broadcast(P)).then_inc(gates_in, 16)
            act.wait_ge(wvu_ld, 16)
            act.dma_start(wvd_in, wvd).then_inc(wvd_ld, 16)

            def value_map(s):
                act.wait_ge(m1_ready, s + 1)
                nc.scalar.activation(m1[:, s, :], banks[4 + s][:, 0:VB], ACT.Copy).then_inc(m1_copied, 1)

            act.wait_ge(scales_ready, 1)
            for blk in range(6):
                w = BOT if blk == 4 else P
                kind = 0 if blk < 4 else blk - 3
                for i in range(4):
                    q = 4 * blk + i
                    act.wait_ge(quad_ready, q + 1)
                    dst = split[:, blk, 0].rearrange("p (k n) -> p k n", k=KC)[:, 4 * i:4 * i + 4, 0:w]
                    nc.scalar.activation(dst, quad[q % 4][:, :, 0:w], ACT.Copy, scale=scl3[:, kind:kind + 1])\
                        .then_inc(quad_hi, 1)
            for blk in range(6, 11):
                if blk >= 7:
                    act.wait_ge(split_stored[blk - 7], 16)
                for i in range(4):
                    q = 4 * blk + i
                    dst = wvdT if blk == 6 else avT[blk - 7]
                    act.wait_ge(quad_ready, q + 1)
                    nc.scalar.activation(dst[:, 4 * i:4 * i + 4, :], quad[q % 4], ACT.Copy).then_inc(quad_copied, 1)
                if blk >= 8:
                    value_map(blk - 8)
            value_map(SC - 1)
            act.wait_ge(s65_stored, 16)
            for blk in (4, 5):
                act.wait_ge(split_stored[blk], 32 if blk == 4 else 16)

            with act.Fori(0, B) as b:
                def normal(h, t):
                    if t < 2:
                        act.wait_ge(kt_ready, 16 * b + 4 * h + 1)
                        act.wait_ge(v_ready, 32 * b + 8 * h + 1)
                    else:
                        act.wait_ge(v_ready, 32 * b + 8 * h + t)
                    nc.scalar.activation(xn[:, t % 2, :], X[:, t, h * HD:(h + 1) * HD], ACT.Identity,
                                         bias=bias1[:, t:t + 1], scale=rstd1[:, t:t + 1]).then_inc(xn_ready, 1)

                def value_high(h, t):
                    act.wait_ge(xn_ready, 32 * b + 8 * h + t + 1)
                    nc.scalar.activation(V[:, h % 2, t, 0, :], xn[:, t % 2, :], ACT.Copy).then_inc(vhi_ready, 1)

                def query(h, c):
                    act.wait_ge(tr_ready, 16 * b + 4 * h + c + 1)
                    nc.scalar.activation(QT[:, 0, c, :], TPH[c % 2], ACT.Copy).then_inc(qhi_ready, 1)
                    nc.scalar.activation(QT[:, 1, c, :], TPL[c % 2], ACT.Copy).then_inc(qlo_ready, 1)

                def sigmoids(h, s):
                    for k in PC_OF[s]:
                        act.wait_ge(scores_ready, 48 * b + NPC * h + k + 1)
                        if h == 0 and k < 3:
                            act.wait_ge(attn_ready, 48 * b + 1)
                        else:
                            act.wait_ge(attn_ready, 48 * b + NPC * h + k - 1)
                        n = PIECES[k][2]
                        nc.scalar.activation(sig[:, k % 3, 0:n], SB[k % 2][:, 0:n], ACT.Sigmoid,
                                             scale=sigscale[:, h:h + 1]).then_inc(sig_ready, 1)
                        act.wait_ge(sig_ready, 48 * b + NPC * h + k + 1)
                        at = PIECES[k][3]
                        nc.scalar.activation(A[:, 0, at:at + n], sig[:, k % 3, 0:n], ACT.Copy, scale=FP16_LIFT)\
                            .then_inc(ahi_ready, 1)

                def scale_ctx(s, j):
                    act.wait_ge(ctx_loaded[j % 2], 16 * (2 * (4 * b + s) + j // 2 + 1))
                    nc.scalar.activation(raw[:, j % 2], raw[:, j % 2], ACT.Identity, bias=Z2, scale=R2S)\
                        .then_inc(ctx_scaled, 1)

                def scale_x(t):
                    if t % 4 == 0:
                        act.wait_ge(affine_ready, 2 * b + t // 4 + 1)
                    if t == 2:
                        act.wait_ge(out_ready, 32 * b + 32)
                    if t >= 4:
                        act.wait_ge(q1_ready, 8 * b + t - 1)
                    nc.scalar.activation(xq[t], X[:, t, :], ACT.Identity, bias=xbias[:, t:t + 1],
                                         scale=xscale[:, t:t + 1]).then_inc(xq_ready, 1)

                def rows_over(t):
                    act.wait_ge(q1tr_ready, 8 * b + t + 1)
                    nc.scalar.activation(q1T[:, t, 0:8, :], TQ[t % 2][0], ACT.Copy)
                    nc.scalar.activation(q1T[:, t, 8:16, :], TQ[t % 2][1], ACT.Copy).then_inc(q1t_ready, 1)

                def store_x2(i):
                    s, a, z = MOVES[i]
                    act.wait_ge(x2_counted, 32 * b + 8 * s + z + 1)
                    act.dma_start(x2_d[bass.ds(b * NT + a, z - a), :, s * 512:(s + 1) * 512]
                                  .rearrange("t p n -> p t n"), X[:, a:z, s * 512:(s + 1) * 512])\
                       .then_inc(x2_stored[i], 16)

                act.wait_ge(norm_ready, b + 1)
                for t in range(NT):
                    normal(0, t)
                for c in range(DC):
                    query(0, c)
                for h in range(H):
                    last = h == H - 1
                    for s in range(NT):
                        sigmoids(h, s)
                        if not last:
                            for t in V_AFTER[s]:
                                normal(h + 1, t)
                            for t in V_AFTER[s]:
                                value_high(h + 1, t)
                        elif s in CTX_AFTER:
                            scale_ctx(*CTX_AFTER[s])
                    if not last:
                        for c in range(DC):
                            query(h + 1, c)
                scale_x(0)
                scale_x(1)
                scale_x(2)
                for t in range(1, NT + 1):
                    rows_over(t - 1)
                    if t + 2 < NT:
                        scale_x(t + 2)
                    if 4 <= t < 6:
                        scale_ctx(1, t - 2)
                for s in range(1, NS):
                    if s > 1:
                        for j in range(4):
                            scale_ctx(s, j)
                    store_x2(s - 1)
                for i in range(NS - 1, len(MOVES)):
                    store_x2(i)

            def high(n, q, g):
                act.wait_ge(ht_tr, 8 * n + g + 2)
                t, k = g // 4, g % 4
                nc.scalar.activation(hT[:, q, 0, 4 * k:4 * k + 4, t * P:(t + 1) * P], quad[g % 2], ACT.Copy)\
                    .then_inc(ht_hi, 1)

            for i in range(len(MOVES)):
                act.wait_ge(x2_stored[i], 16 * B + 1)
            for g in range(8):
                high(0, 0, g)
            act.wait_ge(tab_ready, B)
            nc.scalar.activation(logv, tab[:, 2, :], ACT.Ln, bias=onesf[:, 0:1]).then_inc(log_ready, 1)

            def gelu(n, f):
                act.wait_ge(u_ready, 4 * n + f + 1)
                nc.scalar.activation(gl[:, f % 2, :], banks[3 - f % 2][:, 0:TG * P], ACT.Gelu_apprx_tanh,
                                     bias=bu1s[:, f:f + 1], scale=uns3[:, 0:1]).then_inc(gelu_ready, 1)

            def expo(n, t):
                act.wait_ge(nmx_ready, TG * n + t + 1)
                nc.scalar.activation(ew[:, t, :], am[:, t, :], ACT.Exp, bias=nmx[:, t:t + 1],
                                     accum_out=den[:, t:t + 1]).then_inc(e_ready, 1)

            def gate_and_low(n):
                act.wait_ge(lcol_ready, n + 1)
                nc.scalar.activation(ge[:, 0, :], banks[7][:, 300:300 + TG], ACT.Tanh, scale=0.5,
                                     bias=hbu2).then_inc(e1_ready, 1)
                act.wait_ge(z_ready, n + 1)
                nc.scalar.activation(ge[:, 6, :], ge[:, 5, :], ACT.Tanh, scale=0.5).then_inc(e2_ready, 1)
                act.wait_ge(low_mm, n + 1)
                nc.scalar.activation(low[:, 0, :], banks[7][:, 0:TG * P], ACT.Copy, scale=FP16_LIFT)\
                    .then_inc(low_hi, 1)

            def group(n, q, first, last):
                act.wait_ge(q_ready, n + 1)
                nc.scalar.activation(qT[0:BOT, q, :], banks[2][0:BOT, 0:TG * P], ACT.Copy,
                                     scale=uns3[0:BOT, 1:2]).then_inc(qT_ready, 1)
                if not first:
                    gate_and_low(n - 1)
                for f in range(4):
                    if f < 2:
                        act.wait_ge(lrn_ready, 4 * n + 1)
                    else:
                        act.wait_ge(lrn_ready, 4 * n + f)
                    gelu(n, f)
                    if f % 2:
                        expo(n, f // 2)
                    if f < 2 and not last:
                        for g in range(4 * f, 4 * f + 4):
                            high(n + 1, 1 - q, g)

            group(0, 0, True, False)
            with act.Fori(0, NG // 2 - 1) as i:
                group(2 * i + 1, 1, False, False)
                group(2 * i + 2, 0, False, False)
            group(NG - 1, 1, False, True)
            gate_and_low(NG - 1)

        @block.tensor
        def _(pe):
            pe.sem_inc(ht_tr, 1)
            pe.sem_inc(lrn_ready, 1)
            pe.wait_ge(consts_made, 3)
            pe.wait_ge(consts_cast, 4)
            pe.wait_ge(prep_done, 16 * 2)
            for c in range(SC):
                nc.tensor.transpose(banks[5][0:BOT, c * P:(c + 1) * P], ak_in[:, c, :], identf)
            nc.tensor.transpose(banks[4][0:BOT, 0:RDIM], wr_in[0:RDIM, :], identf[0:RDIM, 0:RDIM]).then_inc(ak_tr, 1)
            pe.wait_ge(ak_copied, 2)
            nc.tensor.matmul(banks[6][0:RDIM, :], wrT[0:BOT, 0:RDIM], akT[0:BOT, :], start=True, stop=True)\
                .then_inc(rk_ready, 1)
            pe.wait_ge(rk_copied, 1)
            nc.tensor.matmul(banks[4][0:BOT, :], wr_in[0:RDIM, :], rkT[0:RDIM, :], start=True, stop=True)\
                .then_inc(m2_ready, 1)
            def value_map(s):
                pe.wait_ge(quad_copied, 4 * s + 8)
                for k in range(KC):
                    last = nc.tensor.matmul(banks[4 + s][:, 0:VB], avT[s][:, k, :], wvdT[:, k, :],
                                            start=k == 0, stop=k == KC - 1)
                last.then_inc(m1_ready, 1)

            blocks = [(wu_ld[f], wu_in[f], P) for f in range(4)] + [(wq_ld, wq_in, BOT), (wvu_ld, None, P),
                      (wvd_ld, wvd_in, P)] + [(av_ld[s], av_in[s], P) for s in range(4)]
            for blk, (loaded, src, rows) in enumerate(blocks):
                if blk == 6:
                    pe.wait_ge(bv_part, 1)
                    nc.tensor.matmul(banks[7][:, 0:2 * H], onesf, part.rearrange("p k h -> p (k h)"),
                                     start=True, stop=True).then_inc(bv_sum, 1)
                pe.wait_ge(loaded, 16)
                for i in range(4):
                    q = 4 * blk + i
                    if q >= 28:
                        pe.wait_ge(quad_copied, q - 27)
                    elif q >= 4:
                        pe.wait_ge(quad_used, q - 3)
                    for k in range(4 * i, 4 * i + 4):
                        chunk = wvu_in[:, k, :] if src is None else src[0:rows, k * P:(k + 1) * P]
                        last = nc.tensor.transpose(quad[q % 4][:, k % 4, 0:rows], chunk, identf[0:rows, 0:rows])
                    last.then_inc(quad_ready, 1)
                if blk == 8:
                    pe.wait_ge(s65_made, 2)
                if blk >= 8:
                    value_map(blk - 8)
            pe.wait_ge(bv_read, 1)
            value_map(SC - 1)
            pe.wait_ge(m1_copied, SC)
            pe.wait_ge(quad_copied, 20)

            with pe.Fori(0, B) as b:
                def turn(h, c):
                    if c == 0:
                        pe.wait_ge(v_ready, 32 * b + 8 * h + 8 + 1)
                    if c >= 2:
                        pe.wait_ge(qlo_ready, 16 * b + 4 * h + c - 1)
                    for l, bank in ((0, TPH), (1, TPL)):
                        for t in range(NT):
                            last = nc.tensor.transpose(bank[c % 2][:, t * P:(t + 1) * P],
                                                       V[:, h % 2, t, l, c * P:(c + 1) * P], ident16)
                    last.then_inc(tr_ready, 1)

                def scores(h, s):
                    for k in PC_OF[s]:
                        _, a, n, _ = PIECES[k]
                        if h == 0 and k < 2:
                            pe.wait_ge(mm_used, 32 * b + 1)
                        else:
                            pe.wait_ge(sig_ready, 48 * b + NPC * h + k - 1)
                        for c in range(DC):
                            if k == 0:
                                pe.wait_ge(kt_ready, 16 * b + 4 * h + c + 2)
                            for i, (lk, lq) in enumerate(((0, 0), (0, 1), (1, 0))):
                                last = nc.tensor.matmul(SB[k % 2][:, 0:n], KT[:, lk, c, s * P:(s + 1) * P],
                                                        QT[:, lq, c, a:a + n], start=c == 0 and i == 0,
                                                        stop=c == DC - 1 and i == 2)
                        last.then_inc(scores_ready, 1)

                def values(h, t):
                    pe.wait_ge(attn_ready, 48 * b + NPC * h + PC_UNTIL[t] + 1)
                    if h == 0 and t < 2:
                        pe.wait_ge(mm_used, 32 * b + 1)
                    else:
                        pe.wait_ge(out_used, 32 * b + 8 * h + t - 1)
                    for s in range(t + 1):
                        a = STORE[s] + (t - s) * P
                        for i, (la, lv) in enumerate(((0, 0), (0, 1), (1, 0))):
                            last = nc.tensor.matmul(PO[t % 2], A[:, la, a:a + P], V[:, h % 2, s, lv, :],
                                                    start=s == 0 and i == 0, stop=s == t and i == 2)
                    last.then_inc(out_ready, 1)

                def turn_x(t):
                    pe.wait_ge(q1_ready, 8 * b + t + 1)
                    if t >= 2:
                        pe.wait_ge(q1t_ready, 8 * b + t - 1)
                    for k in range(KC):
                        last = nc.tensor.transpose(TQ[t % 2][k // 8][:, k % 8, :], q1b[:, t % 2, k * P:(k + 1) * P],
                                                   identb)
                    last.then_inc(q1tr_ready, 1)

                def row_sums(t):
                    pe.wait_ge(q1t_ready, 8 * b + t + 1)
                    if t == 0:
                        pe.wait_ge(out_used, 32 * b + 32)
                    pe.wait_ge(rows_used, 8 * b + t + 1)
                    for k in range(KC):
                        last = nc.tensor.matmul(PO[0][:, t:t + 1], q1T[:, t, k, :], onesb[:, 0:1],
                                                start=k == 0, stop=k == KC - 1)
                    last.then_inc(rows_ready, 1)

                def col_sums(s):
                    pe.wait_ge(q2_ready, 4 * b + s + 1)
                    pe.wait_ge(cb_ready, 4 * b + s + 1)
                    nc.tensor.matmul(PO[1], ones16, tree[:, 0, :], start=True, stop=True).then_inc(cols_ready, 1)

                def product(s, t):
                    if s or t >= 2:
                        pe.wait_ge(mm_used, 32 * b + 8 * s + t )
                    for k in range(KC):
                        last = nc.tensor.matmul(SB[t % 2], q1T[:, t, k, :], Q2[:, s % 2, k, :],
                                                start=k == 0, stop=k == KC - 1)
                    last.then_inc(mm_ready, 1)

                for c in range(DC):
                    turn(0, c)
                for h in range(H):
                    scores(h, 0)
                    scores(h, 1)
                    for s in range(2, NT):
                        scores(h, s)
                        values(h, s - 2)
                    if h < H - 1:
                        turn(h + 1, 0)
                        turn(h + 1, 1)
                        values(h, 6)
                        turn(h + 1, 2)
                        turn(h + 1, 3)
                        values(h, 7)
                    else:
                        values(h, 6)
                        values(h, 7)
                for t in range(NT + 2):
                    if t < NT:
                        turn_x(t)
                    if 1 <= t <= NT:
                        row_sums(t - 1)
                    if t == 2:
                        col_sums(0)
                    if t >= 2:
                        product(0, t - 2)
                for s in range(1, NS):
                    col_sums(s)
                    for t in range(NT):
                        product(s, t)

            def turn_h(n, g, settled=False):
                t, k = g // 4, g % 4
                if g == 0 and not settled:
                    pe.wait_ge(mm_used, 32 * B + 1)
                pe.wait_ge(h_ready, TG * n + t + 1)
                if g in (4, 5) and settled:
                    pe.wait_ge(fin_used, 8 * (n - 1) + 1)
                elif g >= 2:
                    pe.wait_ge(ht_ready, 8 * n + g - 1)
                for i in range(4):
                    kk = 4 * k + i
                    last = nc.tensor.transpose(quad[g % 2][:, i, :], hs[:, t, kk * P:(kk + 1) * P], identf)
                last.then_inc(ht_tr, 1)

            def project(n, q, f, quads=(), settled=True):
                bank, m = (banks[2], BOT) if f < 0 else (banks[3 - f % 2], P)
                for k in range(KC):
                    for i, (lw, lh) in enumerate(((0, 0), (0, 1), (1, 0))):
                        w = WQT[:, lw, k, :] if f < 0 else WT[:, f, lw, k, :]
                        last = nc.tensor.matmul(bank[0:m, 0:TG * P], w, hT[:, q, lh, k, :],
                                                start=k == 0 and i == 0, stop=k == KC - 1 and i == 2)
                    if k % 4 == 3 and k // 4 < len(quads):
                        turn_h(n + 1, quads[k // 4], settled)
                last.then_inc(q_ready if f < 0 else u_ready, 1)

            def slot_scores(n, q, t):
                for r in range(2):
                    last = nc.tensor.matmul(banks[4 + r], qT[0:BOT + 1, q, t * P:(t + 1) * P],
                                            s65[0:BOT + 1, r * NSLOT:(r + 1) * NSLOT], start=True, stop=True)
                last.then_inc(sc_ready, 1)

            def learned(n, f):
                pe.wait_ge(gelu_ready, 4 * n + f + 1)
                nc.tensor.matmul(banks[7][0:1, 0:TG * P], wu2s[:, f:f + 1], gl[:, f % 2, :],
                                 start=f == 0, stop=f == 3).then_inc(lrn_ready, 1)

            def turn_weights(n):
                for t in range(TG):
                    pe.wait_ge(w_ready, TG * n + t + 1)
                    for c in range(SC):
                        last = nc.tensor.transpose(wT_bank[t][:, c, :], ew[:, t, c * P:(c + 1) * P], identf)
                    last.then_inc(wT_tr, 1)

            def learned_columns(n):
                pe.wait_ge(lrow_ready, n + 1)
                for t in range(TG):
                    last = nc.tensor.matmul(banks[7][:, 300 + t:301 + t], lrow[0:1, t * P:(t + 1) * P],
                                            onesf[0:1, 0:1], start=True, stop=True)
                last.then_inc(lcol_ready, 1)

            def low_values(n):
                pe.wait_ge(e1_ready, n + 1)
                pe.wait_ge(wT_ready, TG * n + TG)
                for c in range(SC):
                    last = nc.tensor.matmul(banks[7][:, 0:TG * P], m1[:, c, :], wTt[:, c, :], start=c == 0,
                                            stop=c == SC - 1)
                last.then_inc(low_mm, 1)

            def finish(n, turned=None):
                pe.wait_ge(low_ready, n + 1)
                for i in range(4 * TG):
                    t, s = i // 4, i % 4
                    if i == 2 and turned is not None:
                        pe.wait_ge(ht_ready, turned)
                    if i >= 4:
                        pe.wait_ge(fin_used, 8 * n + i - 2)
                    for j, (ll, lw) in enumerate(((0, 0), (0, 1), (1, 0))):
                        last = nc.tensor.matmul(fin_bank[i % 4], low[:, ll, t * P:(t + 1) * P],
                                                WVUT[:, lw, s * 512:(s + 1) * 512], start=j == 0, stop=j == 2)
                    last.then_inc(fin_ready, 1)

            def group(n, q, first, last_group):
                pe.wait_ge(ht_ready, 8 * n + 8)
                if not first:
                    pe.wait_ge(gelu_ready, 4 * n)
                project(n, q, -1)
                if not first:
                    learned(n - 1, 3)
                    turn_weights(n - 1)
                    pe.wait_ge(sc_used, TG * n)
                pe.wait_ge(qT_ready, n + 1)
                slot_scores(n, q, 0)
                if not first:
                    learned_columns(n - 1)
                project(n, q, 0)
                if not first:
                    low_values(n - 1)
                project(n, q, 1, () if last_group else range(0, 4), not first)
                pe.wait_ge(sc_used, TG * n + 1)
                if not first:
                    finish(n - 1, None if last_group else 8 * (n + 1) + 4)
                learned(n, 0)
                if not first:
                    pe.wait_ge(fin_used, 8 * n - 1)
                slot_scores(n, q, 1)
                pe.wait_ge(gelu_ready, 4 * n + 1)
                project(n, q, 2, () if last_group else range(4, 8), not first)
                learned(n, 1)
                project(n, q, 3)
                learned(n, 2)

            for g in range(8):
                turn_h(0, g)
            pe.wait_ge(lsum_ready, 1)
            pe.wait_ge(mm_used, 32 * B + 1)
            nc.tensor.matmul(banks[7][:, 0:1], onesf, lsum, start=True, stop=True).then_inc(lsum_all, 1)
            pe.wait_ge(w3_loaded, 16 * 4)
            group(0, 0, True, False)
            with pe.Fori(0, NG // 2 - 1) as i:
                group(2 * i + 1, 1, False, False)
                group(2 * i + 2, 0, False, False)
            group(NG - 1, 1, False, True)
            learned(NG - 1, 3)
            turn_weights(NG - 1)
            learned_columns(NG - 1)
            low_values(NG - 1)
            finish(NG - 1)

        @block.vector
        def _(dve):
            order = Order(dve, dve_order)
            link, did = order.link, order.did
            tt, ts, stt = nc.vector.tensor_tensor, nc.vector.tensor_scalar, nc.vector.scalar_tensor_tensor

            for told in (kt_ready, v_ready, x1_ready, x2_ready, mm_used, attn_ready, cb_ready, rows_used, fin_used,
                         x2_counted):
                dve.sem_inc(told, 1)

            nc.vector.memset(ones16, 1.0).then_inc(consts_cast, 1)
            nc.vector.memset(onesb, 1.0).then_inc(consts_cast, 1)
            did(nc.vector.memset(mx3, 0.0))
            dve.wait_ge(consts_made, 3)
            nc.vector.tensor_copy(ident16, identf).then_inc(consts_cast, 1)
            nc.vector.tensor_copy(identb, identf).then_inc(consts_cast, 1)
            did(nc.vector.tensor_copy(mask16, mask))

            def largest(f):
                dve.wait_ge(wu_ld[f], 16)
                did(nc.vector.tensor_reduce(mx[:, f:f + 1], wu_in[f], AX.X, ALU.max, apply_absolute_value=True))

            largest(0)
            largest(1)
            dve.wait_ge(ak_tr, 1)
            nc.vector.tensor_copy(akT[0:BOT, :], banks[5][0:BOT, :]).then_inc(ak_copied, 1)
            nc.vector.tensor_copy(wrT[0:BOT, :], banks[4][0:BOT, 0:RDIM]).then_inc(ak_copied, 1)
            ts(s65p[0:BOT, NSLOT:], banks[5][0:BOT, :], BOT ** -0.5, None, ALU.mult).then_inc(s65_made, 1)
            largest(2)
            dve.wait_ge(rk_ready, 1)
            nc.vector.tensor_copy(rkT[0:RDIM, :], banks[6][0:RDIM, :]).then_inc(rk_copied, 1)
            largest(3)
            dve.wait_ge(m2_ready, 1)
            ts(s65p[0:BOT, 0:NSLOT], banks[4][0:BOT, :], RDIM ** -0.5, None, ALU.mult).then_inc(s65_made, 1)
            dve.wait_ge(wq_ld, 16)
            did(nc.vector.tensor_reduce(mx3[0:BOT, 1:2], wq_in[0:BOT, :], AX.X, ALU.max, apply_absolute_value=True))
            dve.wait_ge(wvu_ld, 16)
            did(nc.vector.tensor_reduce(mx3[:, 2:3], wvu_in.rearrange("p k v -> p (k v)"), AX.X, ALU.max,
                                        apply_absolute_value=True))
            order.wait()
            nc.vector.tensor_reduce(mx3[:, 0:1], mx[:, 0:4], AX.X, ALU.max).then_inc(abs_done, 1)

            def powers(a, z, n):
                dve.wait_ge(absmax_all, n)
                bits = lambda v: v[:, a:z].bitcast(U32)
                link(ts(bits(pw3), bits(gm3), 0x7F800000, None, ALU.bitwise_and))
                link(ts(pw3[:, a:z], pw3[:, a:z], 2.0 ** -100, None, ALU.max))
                did(ts(uns3[:, a:z], pw3[:, a:z], 1.0 / FP16_LIFT, None, ALU.mult))
                link(nc.vector.reciprocal(scl3[:, a:z], pw3[:, a:z]))

            powers(0, 3, 1)
            ts(scl3[:, 0:3], scl3[:, 0:3], FP16_LIFT, None, ALU.mult).then_inc(scales_ready, 1)
            dve.wait_ge(scales_ready, 1)
            for blk in range(6):
                for i in range(4):
                    q = 4 * blk + i
                    w = BOT if blk == 4 else P
                    kind = 0 if blk < 4 else blk - 3
                    lo, hi = [split[:, blk, l].rearrange("p (k n) -> p k n", k=KC)[:, 4 * i:4 * i + 4, 0:w]
                              for l in (1, 0)]
                    dve.wait_ge(quad_hi, q + 1)
                    stt(lo, quad[q % 4][:, :, 0:w], scl3[:, kind:kind + 1], hi, ALU.mult, ALU.subtract)\
                        .then_inc(quad_used, 1)

            dve.wait_ge(small_in, 16 * N_SMALL)
            did(nc.vector.reciprocal(R1S, S1))
            did(nc.vector.reciprocal(R2S, S2))
            did(tt(S12, S1, S2, ALU.mult))
            did(ts(ND1, Z1, -1.0, QMID, ALU.mult, ALU.add))
            did(ts(ND2, Z2, -1.0, QMID, ALU.mult, ALU.add))
            did(ts(hbu2, hbu2, 0.5, None, ALU.mult))
            order.wait()
            did(stt(KDD, ND1, float(D), ND2, ALU.mult, ALU.mult))

            nc.vector.tensor_reduce(part, bqk, AX.X, ALU.add, apply_absolute_value=True).then_inc(bv_part, 1)
            for h in range(H):
                did(nc.vector.tensor_reduce(alpha[:, 2, h:h + 1], vb[:, h, :], AX.X, ALU.add,
                                            apply_absolute_value=True))
            did(ts(sgn, bqk, 0.0, 2.0, ALU.is_ge, ALU.mult))
            order.wait()
            did(ts(sgn, sgn, -1.0, None, ALU.add))
            ts(alpha[:, 2, :], alpha[:, 2, :], 1.0 / HD, None, ALU.mult).then_inc(alpha_ready, 1)
            dve.wait_ge(bv_sum, 1)
            ts(alpha[:, 0:2, :], banks[7][:, 0:2 * H].rearrange("p (k h) -> p k h", h=H), 1.0 / HD, None, ALU.mult)\
                .then_inc(bv_read, 1)
            dve.wait_ge(bv_read, 1)
            for k in range(2):
                for h in range(H):
                    did(ts(btm[:, k, h, :], sgn[:, k, h, :], alpha[:, k, h:h + 1], None, ALU.mult))
            order.wait()
            link(tt(bnd, btm, bqk, ALU.subtract))
            link(tt(bnd, bnd, bqk, ALU.add))
            link(ts(part, alpha[:, 0:2, :], 1e-37, None, ALU.max))
            link(nc.vector.reciprocal(part, part))
            for k in range(2):
                for h in range(H):
                    did(ts(bnd[:, k, h, :], bnd[:, k, h, :], part[:, k, h:h + 1], None, ALU.mult))
            order.wait()
            did(tt(rse[:, 0], bnd[:, 0], bnd[:, 1], ALU.mult))
            link(tt(rse[:, 1], sgn[:, 0], sgn[:, 1], ALU.mult))
            did(tt(rse[:, 2], rse[:, 0], rse[:, 1], ALU.subtract))
            link(tt(sigscale, alpha[:, 0, :], alpha[:, 1, :], ALU.mult))
            link(ts(sigscale, sigscale, 4.0 * HD ** -0.5, None, ALU.mult))
            dve.wait_ge(abs_done, 1)
            dve.wait_ge(alpha_ready, 1)
            dve.wait_ge(gates_in, 16 * 2)
            order.wait()

            order.start()
            with dve.Fori(0, B) as b:
                order.enter(b, DVE_BATCH)

                def count(t, s):
                    return nc.vector.bn_stats(bn[:, t, s, :], X[:, t, s * 512:(s + 1) * 512])

                def inv_dev(a, n, at):
                    order.wait(at)
                    for t in range(a, a + n):
                        if t == a:
                            nc.vector.memset(pause, 0)
                        did(nc.vector.bn_aggr(mv[:, t, :], bn[:, t].rearrange("p s k -> p (s k)")))
                    order.wait()
                    y, v, w = rstd[:, a:a + n], veps[:, 0:n], nwt[:, 0:n]
                    link(ts(v, mv[:, a:a + n, 1], EPS, None, ALU.add))
                    link(ts(y.bitcast(U32), v.bitcast(U32), -0.5, RSQRT_MAGIC, ALU.mult, ALU.add))
                    for _ in range(4):
                        link(tt(w, y, y, ALU.mult))
                        link(stt(w, w, -0.5, v, ALU.mult, ALU.mult))
                        link(stt(y, w, 1.5, y, ALU.add, ALU.mult))

                def value_low(h, t):
                    dve.wait_ge(vhi_ready, 32 * b + 8 * h + t + 1)
                    tt(V[:, h % 2, t, 1, :], xn[:, t % 2, :], V[:, h % 2, t, 0, :], ALU.subtract).then_inc(v_ready, 1)

                def keys(h, c):
                    r, sg, se = [rse[:, i, h, c:c + 1] for i in range(3)]
                    dve.wait_ge(qhi_ready, 16 * b + 4 * h + c + 1)
                    did(ts(KT[:, 0, c, :], QT[:, 0, c, :], sg, None, ALU.mult))
                    dve.wait_ge(qlo_ready, 16 * b + 4 * h + c + 1)
                    if c < 2:
                        dve.wait_ge(v_ready, 32 * b + 8 * h + 8 + 1)
                    else:
                        dve.wait_ge(kt_ready, 16 * b + 4 * h + c )
                    link(ts(ktmp[:, c % 2, :], QT[:, 1, c, :], r, None, ALU.mult))
                    stt(KT[:, 1, c, :], QT[:, 0, c, :], se, ktmp[:, c % 2, :], ALU.mult, ALU.add)\
                        .then_inc(kt_ready, 1)

                def weights(h, s):
                    for i, k in enumerate(PC_OF[s]):
                        _, _, n, at = PIECES[k]
                        dve.wait_ge(ahi_ready, 48 * b + NPC * h + k + 1)
                        lo = stt(A[:, 1, at:at + n], sig[:, k % 3, 0:n], FP16_LIFT, A[:, 0, at:at + n], ALU.mult,
                                 ALU.subtract)
                        if i == 0:
                            link(lo)
                            tt(A[:, 0, at:at + P], A[:, 0, at:at + P], mask16, ALU.mult)
                            lo = tt(A[:, 1, at:at + P], A[:, 1, at:at + P], mask16, ALU.mult)
                        lo.then_inc(attn_ready, 1)

                def attended(h, t):
                    n = 32 * b + 8 * h + t + 1
                    dve.wait_ge(out_ready, n)
                    dve.wait_ge(x1_ready, (32 * b if h == 0 and t < 2 else n - 2) + 1)
                    tt(otmp[:, t % 2, :], PO[t % 2], vb[:, h, :], ALU.mult).then_inc(out_used, 1)
                    dve.wait_ge(out_used, n)
                    xs = X[:, t, h * HD:(h + 1) * HD]
                    tt(xs, xs, otmp[:, t % 2, :], ALU.add).then_inc(x1_ready, 1)
                    dve.wait_ge(x1_ready, n + 1)
                    return did(count(t, h))

                def quant_ctx(s, j):
                    n = 16 * b + 4 * s + j + 1
                    dve.wait_ge(ctx_scaled, n)
                    if j == 0 and s >= 2:
                        dve.wait_ge(mm_ready, 32 * b + 8 * (s - 1))
                    dst = Q2[:, s % 2, 4 * j:4 * j + 4, :].rearrange("p k n -> p (k n)")
                    ts(dst, raw[:, j % 2].rearrange("p k n -> p (k n)"), MAGIC, MAGIC + QMID, ALU.add, ALU.subtract)\
                        .then_inc(raw_used, 1)
                    dve.wait_ge(raw_used, n)
                    did(ts(dst, dst, -QMID, 255.0 - QMID, ALU.max, ALU.min))

                def add_rows(s):
                    order.wait()
                    if s:
                        dve.wait_ge(cols_ready, 4 * b + s)
                    link(tt(tree[:, 0:8, :], Q2[:, s % 2, 0:8, :], Q2[:, s % 2, 8:16, :], ALU.add))
                    link(tt(tree[:, 0:4, :], tree[:, 0:4, :], tree[:, 4:8, :], ALU.add))
                    link(tt(tree[:, 0:2, :], tree[:, 0:2, :], tree[:, 2:4, :], ALU.add))
                    tt(tree[:, 0, :], tree[:, 0, :], tree[:, 1, :], ALU.add).then_inc(q2_ready, 1)

                def affine(a, at):
                    inv_dev(a, 4, at)
                    sc, bi = xscale[:, a:a + 4], xbias[:, a:a + 4]
                    link(ts(sc, rstd[:, a:a + 4], R1S, None, ALU.mult))
                    link(tt(bi, mv[:, a:a + 4, 0], sc, ALU.mult))
                    ts(bi, bi, -1.0, Z1, ALU.mult, ALU.add).then_inc(affine_ready, 1)

                def quant_x(t):
                    dve.wait_ge(xq_ready, 8 * b + t + 1)
                    if t >= 2:
                        dve.wait_ge(q1tr_ready, 8 * b + t - 1)
                    link(ts(q1b[:, t % 2, :], xq[t], MAGIC, MAGIC + QMID, ALU.add, ALU.subtract))
                    ts(q1b[:, t % 2, :], q1b[:, t % 2, :], -QMID, 255.0 - QMID, ALU.max, ALU.min).then_inc(q1_ready, 1)

                def row_term(t):
                    dve.wait_ge(rows_ready, 8 * b + t + 1)
                    ts(cvec[:, t:t + 1], PO[0][:, t:t + 1], ND2, KDD, ALU.mult, ALU.add).then_inc(rows_used, 1)
                    dve.wait_ge(rows_used, 8 * b + t + 2)

                def col_term(s):
                    dve.wait_ge(cols_ready, 4 * b + s + 1)
                    if s < 2:
                        dve.wait_ge(x1_ready, 32 * b + 32 + 1)
                    else:
                        dve.wait_ge(mm_used, 32 * b + 8 * (s - 1) + 1)
                    ts(cb[:, s % 2, :], PO[1], ND1, None, ALU.mult).then_inc(cb_ready, 1)
                    dve.wait_ge(cb_ready, 4 * b + s + 2)

                def crossed(s, t):
                    n = 32 * b + 8 * s + t + 1
                    dve.wait_ge(mm_ready, n)
                    dve.wait_ge(x2_ready, (32 * b if s == 0 and t < 2 else n - 2) + 1)
                    stt(xn[:, t % 2, :], SB[t % 2], cvec[:, t:t + 1], cb[:, s % 2, :], ALU.add, ALU.add)\
                        .then_inc(mm_used, 1)
                    dve.wait_ge(mm_used, n + 1)
                    xs = X[:, t, s * 512:(s + 1) * 512]
                    stt(xs, xn[:, t % 2, :], S12, xs, ALU.mult, ALU.add).then_inc(x2_ready, 1)
                    dve.wait_ge(x2_ready, n + 1)
                    count(t, s).then_inc(x2_counted, 1)

                for i, (s, a, z) in enumerate(MOVES):
                    dve.wait_ge(x_loaded[i], 16 * b + 16)
                    for t in range(a, z):
                        at = did(count(t, s))
                inv_dev(0, NT, at)
                did(nc.vector.tensor_copy(rstd1, rstd))
                link(tt(bias1, mv[:, :, 0], rstd, ALU.mult))
                ts(bias1, bias1, -1.0, None, ALU.mult).then_inc(norm_ready, 1)
                for t in range(NT):
                    dve.wait_ge(xn_ready, 32 * b + t + 1)
                    nc.vector.tensor_copy(V[:, 0, t, 0, :], xn[:, t % 2, :]).then_inc(vhi_ready, 1)
                    value_low(0, t)
                dve.wait_ge(vb_ready, H)
                for c in range(DC):
                    keys(0, c)
                for h in range(H):
                    last = h == H - 1
                    for s in range(NT):
                        weights(h, s)
                        if s >= 3:
                            at = attended(h, s - 3)
                        if not last:
                            for t in V_AFTER[s]:
                                value_low(h + 1, t)
                        elif s in CTX_AFTER:
                            quant_ctx(*CTX_AFTER[s])
                    if last:
                        affine(0, at)
                    attended(h, 5)
                    if not last:
                        keys(h + 1, 0)
                        keys(h + 1, 1)
                        attended(h, 6)
                        keys(h + 1, 2)
                        keys(h + 1, 3)
                        attended(h, 7)
                    else:
                        quant_x(0)
                        attended(h, 6)
                        quant_x(1)
                        at = attended(h, 7)
                        add_rows(0)
                for t in range(2, NT + 3):
                    if t < NT:
                        quant_x(t)
                    if 2 <= t < NT + 2:
                        row_term(t - 2)
                    if t == 2:
                        affine(4, at)
                    if t == 3:
                        col_term(0)
                    if 3 <= t:
                        crossed(0, t - 3)
                    if 4 <= t < 6:
                        quant_ctx(1, t - 2)
                    if t == NT:
                        add_rows(1)
                for s in range(1, NS):
                    col_term(s)
                    for t in range(NT):
                        crossed(s, t)
                        if s < NS - 1:
                            if t < 4:
                                quant_ctx(s + 1, t)
                            if t == 5:
                                add_rows(s + 1)
                dve.wait_ge(x2_counted, 32 * b + 32 + 1)
                inv_dev(0, NT, None)
                link(tt(vh, rstd, rstd, ALU.mult))
                link(tt(vh, vh, mv[:, :, 1], ALU.mult))
                did(nc.vector.tensor_copy(tab[:, 0, bass.ds(b * NT, NT)], mv[:, :, 0]))
                did(nc.vector.tensor_copy(tab[:, 1, bass.ds(b * NT, NT)], rstd))
                link(nc.vector.tensor_copy(tab[:, 2, bass.ds(b * NT, NT)], vh))
                nc.vector.memset(pause, 0).then_inc(tab_ready, 1)
            order.leave(B, DVE_BATCH)

            for q in range(2):
                did(nc.vector.memset(qT[BOT:BOT + 1, q, :], 1.0))
            dve.wait_ge(m1_copied, SC)
            nc.vector.tensor_reduce(mx3[:, 3:4], m1, AX.XY, ALU.max, apply_absolute_value=True).then_inc(abs_done, 1)
            order.start()

            def normal_h(n, q):
                dve.wait_ge(y_ready, TG * n + 1)
                dve.wait_ge(ht_tr, 8 * n + 1)
                link(nc.vector.tensor_copy(cur[:, q, 0:2], tab[:, 0:2, bass.ds(n * TG, TG)]))
                for t in range(TG):
                    dve.wait_ge(y_loaded[2 * q + t], 16 * (turn_of(n, q) + 1))
                    ts(hs[:, t, :], Y[:, q, t, :], cur[:, q, 0, t:t + 1], cur[:, q, 1, t:t + 1], ALU.subtract,
                       ALU.mult).then_inc(h_ready, 1)

            def low_h(n, q, g):
                t, k = g // 4, g % 4
                dve.wait_ge(ht_hi, 8 * n + g + 1)
                tt(hT[:, q, 1, 4 * k:4 * k + 4, t * P:(t + 1) * P], quad[g % 2],
                   hT[:, q, 0, 4 * k:4 * k + 4, t * P:(t + 1) * P], ALU.subtract).then_inc(ht_ready, 1)

            def choose(n, t):
                dve.wait_ge(sc_ready, TG * n + t + 1)
                nc.vector.memset(pause, 0)
                link(nc.vector.max(m8[:, t, :], banks[4]))
                nc.vector.memset(pause, 0)
                link(nc.vector.match_replace(rep, m8[:, t, :], banks[4], LOWEST))
                link(tt(nsel, rep, banks[4], ALU.is_equal))
                stt(am[:, t, :], nsel, FAR, banks[5], ALU.mult, ALU.add).then_inc(sc_used, 1)
                dve.wait_ge(sc_used, TG * n + t + 1)
                nc.vector.tensor_reduce(nmx[:, t:t + 1], am[:, t, :], AX.X, ALU.max, negate=True)\
                    .then_inc(nmx_ready, 1)

            def weigh(n, t):
                dve.wait_ge(e_ready, TG * n + t + 1)
                link(nc.vector.reciprocal(rden[:, t:t + 1], den[:, t:t + 1]))
                ts(ew[:, t, :], ew[:, t, :], rden[:, t:t + 1], None, ALU.mult).then_inc(w_ready, 1)

            def weights_rows(n):
                for t in range(TG):
                    dve.wait_ge(wT_tr, TG * n + t + 1)
                    nc.vector.tensor_copy(wTt[:, :, t * P:(t + 1) * P], wT_bank[t]).then_inc(wT_ready, 1)

            def gate(n, q):
                link(nc.vector.tensor_copy(cur[:, q, 2], tab[:, 2, bass.ds(n * TG, TG)]))
                dve.wait_ge(e1_ready, n + 1)
                link(stt(ge[:, 3, :], ge[:, 0, :], 1.25, cur[:, q, 2, :], ALU.mult, ALU.add))
                link(ts(ge[:, 3, :], ge[:, 3, :], 0.0, 5.0, ALU.max, ALU.min))
                link(ts(ge[:, 3, :], ge[:, 3, :], -0.5, 1.0 / 1.5, ALU.add, ALU.mult))
                link(ts(ge[:, 4, :], ge[:, 3, :], 0.0, 1.0, ALU.max, ALU.min))
                ts(ge[:, 5, :], ge[:, 4, :], gw[:, 0:1], gw[:, 1:2], ALU.mult, ALU.add).then_inc(z_ready, 1)
                dve.wait_ge(e2_ready, n + 1)
                dve.wait_ge(fin_used, 8 * n + 1)
                link(ts(ge[:, 8, :], ge[:, 6, :], 0.5, 0.5, ALU.mult, ALU.add))
                link(stt(ge[:, 9, :], ge[:, 8, :], 0.05, ge[:, 8, :], ALU.is_ge, ALU.mult))
                link(ts(ge[:, 9, :], ge[:, 9, :], gsc, None, ALU.mult))
                dve.wait_ge(low_hi, n + 1)
                stt(low[:, 1, :], banks[7][:, 0:TG * P], FP16_LIFT, low[:, 0, :], ALU.mult, ALU.subtract)\
                    .then_inc(low_ready, 1)

            def finish(n, q):
                for i in range(4 * TG):
                    t, s = i // 4, i % 4
                    if s == 0:
                        dve.wait_ge(y_ready, TG * n + t + 2)
                    dve.wait_ge(fin_ready, 8 * n + i + 1)
                    fs = F[:, q, t, s * 512:(s + 1) * 512]
                    stt(fs, fin_bank[i % 4], ge[:, 9, t:t + 1], fs, ALU.mult, ALU.add).then_inc(fin_used, 1)

            def learned_row(n):
                dve.wait_ge(lrn_ready, 4 * n + 5)
                nc.vector.tensor_copy(lrow[0:1, :], banks[7][0:1, 0:TG * P]).then_inc(lrow_ready, 1)

            def group(n, q, first, last_group):
                if not last_group:
                    normal_h(n + 1, 1 - q)
                if not first:
                    learned_row(n - 1)
                    weights_rows(n - 1)
                choose(n, 0)
                if not first:
                    gate(n - 1, 1 - q)
                if not last_group:
                    for g in range(0, 4):
                        low_h(n + 1, 1 - q, g)
                if not first:
                    finish(n - 1, 1 - q)
                choose(n, 1)
                weigh(n, 0)
                if not last_group:
                    for g in range(4, 8):
                        low_h(n + 1, 1 - q, g)
                weigh(n, 1)

            turn = [0]

            def turn_of(n, q):
                return n // 2 if isinstance(n, int) else turn[0] + 1

            normal_h(0, 0)
            for g in range(8):
                low_h(0, 0, g)
            dve.wait_ge(log_ready, 1)
            nc.vector.tensor_reduce(lsum, logv, AX.X, ALU.add).then_inc(lsum_ready, 1)
            dve.wait_ge(lsum_all, 1)
            link(ts(lmean, banks[7][:, 0:1], 1.0 / (B * T), 1e-6, ALU.mult, ALU.add))
            link(nc.vector.reciprocal(lmean, lmean))
            link(ts(tab[:, 2, :], logv, lmean, 0.5, ALU.mult, ALU.mult))
            link(ts(tab[:, 2, :], tab[:, 2, :], 1.25, None, ALU.add))
            powers(3, 4, 2)
            link(ts(m1, m1, scl3[:, 3:4], None, ALU.mult))
            link(tt(gsc, uns3[:, 2:3], uns3[:, 3:4], ALU.mult))
            group(0, 0, True, False)
            order.start()
            with dve.Fori(0, NG // 2 - 1) as i:
                order.enter(i, DVE_PAIR)
                turn[0] = i
                group(2 * i + 1, 1, False, False)
                group(2 * i + 2, 0, False, False)
            order.leave(NG // 2 - 1, DVE_PAIR)
            group(NG - 1, 1, False, True)
            learned_row(NG - 1)
            weights_rows(NG - 1)
            gate(NG - 1, 1)
            finish(NG - 1, 1)


_INS = ['x', 'ctx_4096', 'L0_attn_bv_q', 'L0_attn_bv_k', 'L0_attn_bv_v', 'L0_xattn_x1_scale', 'L0_xattn_x1_zp',
        'L0_xattn_x2_scale', 'L0_xattn_x2_zp', 'L0_ffn_Wq', 'L0_ffn_Wr', 'L0_ffn_aux_keys', 'L0_ffn_aux_values',
        'L0_ffn_Wvd', 'L0_ffn_Wvu', 'L0_ffn_Wu1', 'L0_ffn_bu1', 'L0_ffn_Wu2', 'L0_ffn_bu2', 'L0_ffn_gate_w1',
        'L0_ffn_gate_bias', 'L0_ffn_log_rel']


def kernel(**inputs):
    import numpy as _np
    import concourse.bacc as _bacc
    from concourse import mybir as _mybir
    from concourse.bass_utils import run_bass_kernel_spmd as _run

    nc = _bacc.Bacc("TRN2", target_bir_lowering=False, num_devices=1)
    arrays, args = {}, []
    for name in _INS:
        a = _np.ascontiguousarray(inputs[name])
        arrays[f"in_{name}_dram"] = a
        args.append(nc.dram_tensor(f"in_{name}_dram", a.shape, _mybir.dt.from_np(a.dtype), kind="ExternalInput").ap())
    args.append(nc.dram_tensor("out_0_dram", (B, T, D), F32, kind="ExternalOutput").ap())
    nc.disable_value_cache = True
    decoder_kernel(nc, *args)
    r = _run(nc, [arrays], core_ids=[0])
    return r.results[0]["out_0_dram"]
```
